# Optimizing a Trainium2 kernel written in Bass

```python
import numpy as np
import jax
import jax.numpy as jnp

def _softmax(x, axis=-1):
    return jax.nn.softmax(x, axis=axis)

def _gelu(x):
    return jax.nn.gelu(x, approximate=True)

def _silu(x):
    return jax.nn.silu(x)

def _sigmoid(x):
    return jax.nn.sigmoid(x)

def _layernorm(x, axis=-1, eps=1e-05):
    m = jnp.mean(x, axis=axis, keepdims=True)
    v = jnp.var(x, axis=axis, keepdims=True)
    return (x - m) / jnp.sqrt(v + eps)

def _scatter_add(tgt, idx, src, axis=0):
    return tgt.at[idx].add(src)

def _segment_sum(src, seg, n):
    return jax.ops.segment_sum(src, seg, n)
kernel_name = 'mk_gnn_ffn_d1_gnn_r8_a0ba56'

def setup_inputs(seed: int=0):
    np.random.seed(seed)
    _w = jnp.asarray

    def _rec_inputs():
        import jax
        import jax.numpy as jnp
        _gk = jax.random.key(seed)
        x = -6.415e-05 + 1 * jax.random.normal(jax.random.fold_in(_gk, 1), (1250, 512), jnp.float32)
        _s = jax.random.randint(jax.random.fold_in(_gk, 2), (10000,), 0, 1250, jnp.int32)
        _d = jax.random.randint(jax.random.fold_in(_gk, 3), (10000,), 0, 1250, jnp.int32)
        _loop = jnp.arange(1250, dtype=jnp.int32)
        src = jnp.concatenate([_s, _d, _loop])
        dst = jnp.concatenate([_d, _s, _loop])
        _o = jnp.argsort(dst, stable=True)
        src = src[_o]
        dst = dst[_o]
        edge_attr_512 = -8.16379e-05 + 0.999858 * jax.random.normal(jax.random.fold_in(_gk, 12), (21250, 512), jnp.float32)
        return (x, src, dst, edge_attr_512)
    x, src, dst, edge_attr_512 = _rec_inputs()

    def _L0_gnn_setup():
        import jax, jax.numpy as jnp
        import numpy as np
        N_NODES = 2500
        N_EDGES = 25000
        N_SEG = 16
        EXTENT = 32
        N_PATHS = 64
        OP_SIZE = N_SEG * EXTENT
        key = jax.random.key(seed)
        k1, k2, k3, k4, k5, k6 = jax.random.split(key, 6)
        x_nodes = jax.random.normal(k1, (N_NODES, OP_SIZE), dtype=jnp.float32)
        x_edges = jax.random.normal(k2, (N_EDGES, OP_SIZE), dtype=jnp.float32)
        path_coeffs = jax.random.normal(k3, (N_PATHS,), dtype=jnp.float32)
        src = jax.random.randint(k4, (N_EDGES,), 0, N_NODES, dtype=jnp.int64)
        dst = jax.random.randint(k5, (N_EDGES,), 0, N_NODES, dtype=jnp.int64)
        path_indices = jax.random.randint(k6, (N_PATHS, 3), 0, N_SEG, dtype=jnp.int64)
        return {'x_nodes': x_nodes, 'x_edges': x_edges, 'path_coeffs': path_coeffs, 'src': src, 'dst': dst, 'path_indices': path_indices}
    _L0_gnn_all = _L0_gnn_setup()
    _L0_gnn_in = {k: v for k, v in _L0_gnn_all.items() if k in ('path_coeffs', 'path_indices')}
    del _L0_gnn_all

    def _L0_ffn_setup():
        import jax, jax.numpy as jnp
        import numpy as np
        FP8_MAX = 448.0
        K, N = (512, 512)
        key = jax.random.key(seed)
        kx, kw = jax.random.split(key)
        x = jax.random.normal(kx, (8, 1024, K), dtype=jnp.float32)
        weight = jax.random.normal(kw, (K, N), dtype=jnp.float32) * 0.02
        return {'x': x, 'weight': weight}
    _L0_ffn_all = _L0_ffn_setup()
    _L0_ffn_in = {k: v for k, v in _L0_ffn_all.items() if k in ('weight',)}
    del _L0_ffn_all
    return {'x': x, 'src': src, 'dst': dst, 'edge_attr_512': edge_attr_512, 'L0_gnn_path_coeffs': _L0_gnn_in['path_coeffs'], 'L0_gnn_path_indices': _L0_gnn_in['path_indices'], 'L0_ffn_weight': _L0_ffn_in['weight']}

def reference(x, src, dst, edge_attr_512, L0_gnn_path_coeffs, L0_gnn_path_indices, L0_ffn_weight):
    import jax
    import jax.numpy as jnp

    def _L0_gnn_ref(x_nodes, x_edges, path_coeffs, src, dst, path_indices):
        import jax, jax.numpy as jnp
        import numpy as np
        N_NODES = 2500
        N_EDGES = 25000
        N_SEG = 16
        EXTENT = 32
        N_PATHS = 64
        OP_SIZE = N_SEG * EXTENT
        n_nodes = x_nodes.shape[0]
        x1 = x_nodes[src].reshape(-1, N_SEG, EXTENT)
        x2 = x_edges.reshape(-1, N_SEG, EXTENT)
        i1, i2, i3 = (path_indices[:, 0], path_indices[:, 1], path_indices[:, 2])
        contrib = path_coeffs[None, :, None] * x1[:, i1, :] * x2[:, i2, :]
        edge_out = jnp.zeros((x2.shape[0], N_SEG, EXTENT), x_nodes.dtype).at[:, i3, :].add(contrib)
        out = jnp.zeros((n_nodes, OP_SIZE), x_nodes.dtype).at[dst].add(edge_out.reshape(-1, OP_SIZE))
        return out

    def _L0_ffn_ref(x, weight):
        import jax, jax.numpy as jnp
        import numpy as np
        FP8_MAX = 448.0
        K, N = (512, 512)
        B, S, _ = x.shape
        x2d = x.reshape(-1, K)
        x_amax = jnp.max(jnp.abs(x2d))
        x_scale = FP8_MAX / jnp.maximum(x_amax, 1e-12)
        x_fp8 = jnp.clip(x2d * x_scale, -FP8_MAX, FP8_MAX).astype(jnp.float8_e4m3fn)
        w_amax = jnp.max(jnp.abs(weight))
        w_scale = FP8_MAX / jnp.maximum(w_amax, 1e-12)
        w_fp8 = jnp.clip(weight.T * w_scale, -FP8_MAX, FP8_MAX).astype(jnp.float8_e4m3fn)
        res = jnp.matmul(x_fp8.astype(jnp.float32), w_fp8.astype(jnp.float32).T)
        out = res * (1.0 / x_scale * (1.0 / w_scale))
        return out.reshape(B, S, N).astype(x.dtype)
    x = x + _L0_gnn_ref(_layernorm(x, axis=-1), edge_attr_512, L0_gnn_path_coeffs, src, dst, L0_gnn_path_indices)
    x = x + _L0_ffn_ref(_layernorm(x, axis=-1)[None], L0_ffn_weight)[0]
    return x

_drawn_inputs = setup_inputs


def setup_inputs(seed=0):
    import zlib

    import numpy as np

    out = dict(_drawn_inputs(seed))
    spreads = {}
    factors = {}
    for name, (base, spread) in spreads.items():
        noise = np.random.default_rng([zlib.crc32(name.encode()), seed]).standard_normal(out[name].shape)
        drawn = base * np.exp(spread * noise) if base else spread * noise
        out[name] = jnp.asarray(drawn.astype(out[name].dtype))
    for name, factor in factors.items():
        out[name] = (out[name] * factor).astype(out[name].dtype)
    return out
```

```python
import concourse.bass as bass
from concourse import mybir
from concourse.alu_op_type import AluOpType as ALU
from contextlib import ExitStack

NODES, EDGES, DIM, PATHS = 1250, 21250, 512, 64
SEGS, EXT = 16, 32
P = 128
QUARTERS, EIGHTH = 4, 8
QCOLS = SEGS * EIGHTH
WIN = 32
WIN_TILES, GROUP_TILES = 3, 12
GROUP_WINS = GROUP_TILES // WIN_TILES
FULL_TILES = EDGES // P
TAIL = EDGES - FULL_TILES * P
GROUPS = -(-(FULL_TILES + 1) // GROUP_TILES)
TILES = GROUPS * GROUP_TILES
WINS = TILES // WIN_TILES
PAIRS = GROUPS // 2
MAIN_TILES = 10
CHUNK = 16
CHUNKS = PATHS // CHUNK
BODY_CHUNKS = 2 * CHUNKS
AHEAD = 1
GEN_PASSES = -(-NODES // WIN)
TABLE_ROWS = NODES + WIN
NT = 10
LAST = NODES - (NT - 1) * P
FP8_MAX = 448.0
F32_ROUND = 1.5 * 2.0 ** 20


def gnn_ffn(nc, x, x_quarters, edges, src_t, dst_t, paths, i3_rep, coef_rep, weight_q,
            ident_c, cols_c, elem_c, out):
    fp32, bf16, i32 = mybir.dt.float32, mybir.dt.bfloat16, mybir.dt.int32
    ACT = mybir.ActivationFunctionType
    AX = mybir.AxisListType.X

    ctx = ExitStack()
    with ctx:
        def sb(name, shape, dt=fp32):
            return ctx.enter_context(nc.sbuf_tensor(name, shape, dt))

        def pb(name, shape, dt=fp32):
            return ctx.enter_context(nc.psum_tensor(name, shape, dt))

        def sem(name):
            return ctx.enter_context(nc.semaphore(name))

        xn_dram = nc.dram_tensor("xn_dram", [NODES, DIM], fp32, kind="Internal").ap()
        table = nc.dram_tensor("sum_table", [QUARTERS, TABLE_ROWS, QCOLS], fp32, kind="Internal").ap()

        x1 = [sb(f"x1_{b}", [P, GROUP_TILES, DIM]) for b in range(2)]
        x2 = [sb(f"x2_{b}", [P, GROUP_TILES, DIM]) for b in range(2)]
        prod = [sb(f"prod_{s}", [P, GROUP_TILES, CHUNK, EXT]) for s in range(2)]
        onehot = [sb(f"onehot_{b}", [P, GROUP_TILES, WIN]) for b in range(2)]
        src_slot = [sb(f"src_slot_{b}", [P, GROUP_TILES], i32) for b in range(2)]
        sums = [sb(f"sums_{s}", [P, GROUP_WINS, CHUNK * EIGHTH]) for s in range(2)]
        sums_T = [sb(f"sums_T_{s}", [P, GROUP_WINS, P]) for s in range(2)]
        rows = [sb(f"rows_{b}", [P, GROUP_WINS, QCOLS]) for b in range(2)]
        src_sb = sb("src_sb", [P, TILES], i32)
        dst_sb = sb("dst_sb", [P, TILES], i32)
        dst_f = sb("dst_f", [P, TILES])
        rel_near = sb("rel_near", [P, TILES])
        rel_far = sb("rel_far", [P, TILES])
        outside = sb("outside", [P, TILES])
        above = sb("above", [P, TILES])
        outside_n = sb("outside_n", [P, 1])
        far_flag = sb("far_flag", [1, 1], i32)
        row_near = sb("row_near", [1, WINS], i32)
        row_far_f = sb("row_far_f", [1, WINS])
        row_far = sb("row_far", [1, WINS], i32)
        paths_sb = sb("paths_sb", [1, PATHS, 3], i32)
        off_a = sb("off_a", [1, PATHS])
        packed_f = sb("packed_f", [1, PATHS])
        packed = sb("packed", [1, PATHS], i32)
        i3_sb = sb("i3_sb", [P, CHUNKS], i32)
        coef_sb = sb("coef_sb", [P, CHUNKS])
        i3_col = sb("i3_col", [P, CHUNKS])
        combine = sb("combine", [P, CHUNKS, QCOLS])
        ident = sb("ident", [P, P])
        ident_b = sb("ident_b", [P, P], bf16)
        cols = sb("cols", [P, P])
        elem = sb("elem", [P, 2])
        ones = sb("ones", [P, P])
        zeros = sb("zeros", [P, QCOLS])
        stats = sb("stats", [P, NT, 6])
        mv = sb("mv", [P, NT, 2])
        var_e = sb("var_e", [P, NT])
        std = sb("std", [P, NT])
        inv = sb("inv", [P, NT])
        quot = sb("quot", [P, NT])
        rstd = sb("rstd", [P, NT])
        wq = sb("wq", [P, QUARTERS, DIM], bf16)
        mx = sb("mx", [P, 2])
        mx_all = sb("mx_all", [1, 2])
        mx_bc = sb("mx_bc", [P, 2])
        mx_inv = sb("mx_inv", [P, 2])
        scale = sb("scale", [P, 2])
        scale_inv = sb("scale_inv", [P, 2])
        out_scale = sb("out_scale", [P, 1])
        nodes0 = prod[0][:, :, :, :].rearrange("p t q e -> p (t q e)")[:, 0:NT * DIM]\
            .rearrange("p (t c) -> p t c", c=DIM)
        normed0 = prod[1][:, :, :, :].rearrange("p t q e -> p (t q e)")[:, 0:NT * DIM]\
            .rearrange("p (t c) -> p t c", c=DIM)
        w_sb, w_tmp, w_exp = (sb(name, [P, QUARTERS, DIM])[:, :, :] for name in ("w_sb", "w_tmp", "w_exp"))
        nodes1 = x1[0][:, 0:NT, :]
        y = x2[0][:, 0:NT, :]
        tmp = x2[1][:, 0:NT, :]
        yq = prod[0][:, :, :, :].rearrange("p t q e -> p (t q e)")[:, 0:NT * DIM // 2]\
            .bitcast(bf16).rearrange("p (t c) -> p t c", c=DIM)
        yqT = prod[0][:, :, :, :].rearrange("p t q e -> p (t q e)")[:, NT * DIM // 2:NT * DIM]\
            .bitcast(bf16).rearrange("p (t k c) -> p t k c", k=4, c=P)
        res = normed0

        acc = [pb(f"acc_{s}", [P, GROUP_WINS, CHUNK * EIGHTH]) for s in range(2)]
        turn = [pb(f"turn_{s}", [P, GROUP_WINS, P]) for s in range(2)]
        comb = [pb(f"comb_{b}", [P, GROUP_WINS, QCOLS]) for b in range(2)]
        small = pb("small", [P, 512])
        turn_b = [turn[s][:, :, :].rearrange("p w c -> p (w c)")[:, 0:2 * P].bitcast(bf16)
                  .rearrange("p (q c) -> p q c", q=QUARTERS) for s in range(2)]

        s_const = sem("s_const")
        s_nodes = sem("s_nodes")
        s_idx = sem("s_idx")
        s_weight = sem("s_weight")
        s_init = sem("s_init")
        s_dve = sem("s_dve")
        s_var = sem("s_var")
        s_std = sem("s_std")
        s_normed = sem("s_normed")
        s_normed_out = sem("s_normed_out")
        s_dstf = sem("s_dstf")
        s_base = sem("s_base")
        s_outside = sem("s_outside")
        s_outside_sum = sem("s_outside_sum")
        s_ready = sem("s_ready")
        s_combine = sem("s_combine")
        s_table_init = sem("s_table_init")
        s_zero = sem("s_zero")
        s_x1 = [sem(f"s_x1_{b}") for b in range(2)]
        s_x2 = [sem(f"s_x2_{b}") for b in range(2)]
        s_src = sem("s_src")
        s_onehot = [sem(f"s_onehot_{b}") for b in range(2)]
        s_prod = [sem(f"s_prod_{s}") for s in range(2)]
        s_scattered = [sem(f"s_scattered_{s}") for s in range(2)]
        s_sums = [sem(f"s_sums_{s}") for s in range(2)]
        s_turned = [sem(f"s_turned_{s}") for s in range(2)]
        s_sums_T = [sem(f"s_sums_T_{s}") for s in range(2)]
        s_combined = [sem(f"s_combined_{b}") for b in range(2)]
        s_rows = [sem(f"s_rows_{b}") for b in range(2)]
        s_added = [sem(f"s_added_{b}") for b in range(2)]
        s_rows_free = [sem(f"s_rows_free_{b}") for b in range(2)]
        s_far = sem("s_far")
        s_waited_pool = sem("s_waited_pool")
        s_waited_dve = sem("s_waited_dve")
        s_table_done = sem("s_table_done")
        s_pass = sem("s_pass")
        s_back = sem("s_back")
        s_zrow = sem("s_zrow")
        s_wmax = sem("s_wmax")
        s_mxT = sem("s_mxT")
        s_mx1 = sem("s_mx1")
        s_mxb = sem("s_mxb")
        s_idb = sem("s_idb")
        s_yq = sem("s_yq")
        s_yT = sem("s_yT")
        s_yTc = sem("s_yTc")
        s_mm = sem("s_mm")
        s_res = sem("s_res")
        s_out = sem("s_out")

        block = ctx.enter_context(nc.Block())

        def branch_on(eng, near, far):
            flag = eng.alloc_register("flag")
            eng.load(flag, far_flag[0:1, 0:1])
            with eng.If_eq(flag, 0):
                near()
            with eng.Else():
                with eng.Fori(0, GEN_PASSES) as p:
                    far(p)
            eng.nop()

        @block.sync
        def _(sp):
            sp.dma_start(nodes0[:, 0:NT - 1, :],
                         x[0:(NT - 1) * P, :].rearrange("(t p) c -> p t c", p=P)).then_inc(s_nodes, 16)
            sp.wait_ge(s_zrow, 1)
            sp.dma_start(nodes0[0:LAST, NT - 1, :], x[(NT - 1) * P:NODES, :]).then_inc(s_nodes, 16)
            sp.dma_start(table[:, 0:NODES, :], x_quarters).then_inc(s_table_init, 16)
            sp.wait_ge(s_zero, 1)
            for q in range(QUARTERS):
                sp.dma_start(table[q, NODES:TABLE_ROWS, :], zeros[0:WIN, :]).then_inc(s_table_init, 16)

            def load(g, b, tail=False):
                row = g * (GROUP_TILES * P)
                sp.dma_start(x2[b][:, 0:MAIN_TILES, :],
                             edges[bass.ds(row, MAIN_TILES * P), :].rearrange("(t p) c -> p t c", p=P))\
                    .then_inc(s_x2[b], 16)
                if not tail:
                    sp.dma_start(x2[b][:, MAIN_TILES:GROUP_TILES, :],
                                 edges[bass.ds(row + MAIN_TILES * P, 2 * P), :]
                                 .rearrange("(t p) c -> p t c", p=P)).then_inc(s_x2[b], 16)
                else:
                    sp.dma_start(x2[b][:, MAIN_TILES:GROUP_TILES, :],
                                 edges[EDGES - P:EDGES, :].rearrange("(o p) c -> p o c", o=1)
                                 .broadcast_to((P, 2, DIM))).then_inc(s_x2[b], 16)

            def edge_pass(n):
                sp.wait_ge(s_prod[1], n * (PAIRS * CHUNKS) + AHEAD)
                for b in range(2):
                    load(b, b)

                def step(it):
                    for b in range(2):
                        sp.wait_ge(s_prod[1], AHEAD + (n * PAIRS + it) * CHUNKS + (2 * b - 2))
                        load(2 * it + b, b)
                with sp.Fori(1, PAIRS - 1) as it:
                    step(it)
                for b in range(2):
                    sp.wait_ge(s_prod[1], AHEAD + (n * PAIRS + PAIRS - 1) * CHUNKS + (2 * b - 2))
                    load(GROUPS - 2 + b, b, tail=(b == 1))

            sp.wait_ge(s_ready, 1)
            branch_on(sp, lambda: edge_pass(0), edge_pass)

            sp.wait_ge(s_table_done, 1)
            for q in range(QUARTERS):
                sp.dma_start(nodes1[:, 0:NT - 1, q * QCOLS:(q + 1) * QCOLS],
                             table[q, 0:(NT - 1) * P, :].rearrange("(t p) c -> p t c", p=P)).then_inc(s_back, 16)
            sp.wait_ge(s_zrow, 2)
            for q in range(QUARTERS):
                sp.dma_start(nodes1[0:LAST, NT - 1, q * QCOLS:(q + 1) * QCOLS],
                             table[q, (NT - 1) * P:NODES, :]).then_inc(s_back, 16)
            for t in range(NT):
                sp.wait_ge(s_res, t + 1)
                n = P if t < NT - 1 else LAST
                sp.dma_start(out[t * P:t * P + n, :], res[0:n, t, :]).then_inc(s_out, 16)
            sp.wait_ge(s_out, 16 * NT)

        @block.gpsimd
        def _(pool):
            def take_wait():
                pool.sem_inc(s_waited_pool, 1)

            def indices(g, b):
                nc.gpsimd.tensor_copy(src_slot[b][:, :], src_sb[:, bass.ds(g * GROUP_TILES, GROUP_TILES)])\
                    .then_inc(s_src, 1)

            def gather(n, it, b):
                pool.wait_ge(s_src, (n * PAIRS + it) * 2 + (b + 1))
                take_wait()
                for t in range(GROUP_TILES):
                    nc.gpsimd.indirect_dma_start(
                        out=x1[b][:, t, :], out_offset=None, in_=xn_dram,
                        in_offset=bass.IndirectOffsetOnAxis(ap=src_slot[b][:, t:t + 1], axis=0))\
                        .then_inc(s_x1[b], 16)

            def add_rows(n, it, b, row_of, regs):
                pool.load(regs, row_of[0:1, bass.ds((2 * it + b) * GROUP_WINS, GROUP_WINS)])
                k = n * PAIRS + it
                pool.wait_ge(s_rows[b], AHEAD + k + 1)
                for w in range(GROUP_WINS):
                    row = pool.snap(regs[w], min_val=0, max_val=TABLE_ROWS - WIN)
                    pool.dma_start(table[:, bass.ds(row, WIN), :], rows[b][:, w, :], accum_op=ALU.add)\
                        .then_inc(s_added[b], 16)
                    pool.wait_ge(s_added[b], k * (16 * GROUP_WINS) + 16 * (w + 1))
                    if w < GROUP_WINS - 1:
                        take_wait()
                pool.sem_inc(s_rows_free[b], 1)

            def edge_pass(n, row_of, regs):
                for b in range(2):
                    indices(b, b)
                    gather(n, 0, b)
                with pool.Fori(1, PAIRS) as it:
                    for b in range(2):
                        k = n * PAIRS + it
                        pool.wait_ge(s_prod[1], AHEAD + k * CHUNKS + (2 * b - 2))
                        take_wait()
                        indices(2 * it + b, b)
                        gather(n, it, b)
                        add_rows(n, it - 1, b, row_of, regs)
                for b in range(2):
                    add_rows(n, PAIRS - 1, b, row_of, regs)

            for b in range(2):
                pool.sem_inc(s_rows_free[b], AHEAD)
            nc.gpsimd.memset(zeros[:, :], 0.0).then_inc(s_zero, 1)
            nc.gpsimd.memset(row_far_f[:, :], 0.0).then_inc(s_far, 1)
            pool.wait_ge(s_far, 1)
            nc.gpsimd.tensor_copy(row_far[:, :], row_far_f[:, :]).then_inc(s_far, 1)
            pool.wait_ge(s_idx, 16 * 2)
            pool.wait_ge(s_const, 16 * 3)
            pool.wait_ge(s_ready, 1)
            pool.wait_ge(s_far, 2)
            pool.wait_ge(s_normed_out, 16 * 2)
            pool.wait_ge(s_table_init, 16 * (1 + QUARTERS))
            regs = [pool.alloc_register(f"row_{w}") for w in range(GROUP_WINS)]

            def near():
                edge_pass(0, row_near, regs)

            def far(p):
                edge_pass(p, row_far, regs)
                nc.gpsimd.tensor_scalar(rel_far[:, :], rel_far[:, :], float(-WIN), None, ALU.add).then_inc(s_far, 1)
                nc.gpsimd.tensor_scalar(row_far_f[:, :], row_far_f[:, :], float(WIN), None, ALU.add)\
                    .then_inc(s_far, 1)
                pool.wait_ge(s_far, p * 3 + 4)
                take_wait()
                nc.gpsimd.tensor_copy(row_far[:, :], row_far_f[:, :]).then_inc(s_far, 1)
                pool.wait_ge(s_far, p * 3 + 5)

            branch_on(pool, near, far)
            pool.nop().then_inc(s_table_done, 1)

        @block.vector
        def _(dve):
            chain = [0]

            def link(ins):
                chain[0] += 1
                ins.then_inc(s_dve, 1)
                dve.wait_ge(s_dve, chain[0])

            def layer_stats(nodes, t):
                link(nc.vector.bn_stats(stats[:, t, :], nodes[:, t, :]))
                nc.vector.bn_aggr(mv[:, t, :], stats[:, t, :]).then_inc(s_dve, 1)
                chain[0] += 1

            def rstd_of(k):
                dve.wait_ge(s_dve, chain[0])
                nc.vector.tensor_scalar(var_e[:, :], mv[:, :, 1], 1e-5, None, ALU.add).then_inc(s_var, 1)
                dve.wait_ge(s_std, k)
                link(nc.vector.reciprocal(inv[:, :], std[:, :]))
                link(nc.vector.tensor_tensor(quot[:, :], var_e[:, :], inv[:, :], ALU.mult))
                link(nc.vector.tensor_tensor(quot[:, :], quot[:, :], std[:, :], ALU.add))
                link(nc.vector.tensor_scalar(quot[:, :], quot[:, :], 0.5, None, ALU.mult))
                link(nc.vector.reciprocal(rstd[:, :], quot[:, :]))

            def fp8_scale(k):
                link(nc.vector.tensor_scalar(mx_bc[:, k:k + 1], small[:, k:k + 1], 1e-12, None, ALU.max))
                link(nc.vector.reciprocal(mx_inv[:, k:k + 1], mx_bc[:, k:k + 1]))
                link(nc.vector.tensor_scalar(scale[:, k:k + 1], mx_inv[:, k:k + 1], FP8_MAX, None, ALU.mult))
                link(nc.vector.reciprocal(scale_inv[:, k:k + 1], scale[:, k:k + 1]))

            def to_fp8(src, t1, t2, dst, k):
                link(nc.vector.tensor_scalar(t1, src, scale[:, k:k + 1], FP8_MAX, ALU.mult, ALU.min))
                link(nc.vector.tensor_scalar(t1, t1, -FP8_MAX, None, ALU.max))
                link(nc.vector.tensor_scalar(t2.bitcast(i32), t1.bitcast(i32), 0x7F800000, None, ALU.bitwise_and))
                link(nc.vector.tensor_scalar(t2, t2, 2.0 ** -6, F32_ROUND, ALU.max, ALU.mult))
                link(nc.vector.tensor_tensor(t1, t1, t2, ALU.add))
                return nc.vector.tensor_tensor(dst, t1, t2, ALU.subtract)

            for s in range(2):
                dve.sem_inc(s_prod[s], AHEAD)
            nc.vector.memset(nodes0[96:P, NT - 1, :], 0.0).then_inc(s_zrow, 1)
            link(nc.vector.memset(ones[:, :], 1.0))
            dve.wait_ge(s_idx, 16 * 2)
            nc.vector.tensor_copy(dst_f[:, :], dst_sb[:, :]).then_inc(s_dstf, 1)
            dve.wait_ge(s_nodes, 32)
            for t in range(NT):
                layer_stats(nodes0, t)
            rstd_of(1)
            for t in range(NT):
                last = nc.vector.tensor_scalar(normed0[:, t, :], nodes0[:, t, :], mv[:, t, 0:1], rstd[:, t:t + 1],
                                               ALU.subtract, ALU.mult)
            last.then_inc(s_normed, 1)

            dve.wait_ge(s_const, 16 * 3)
            dve.wait_ge(s_base, 1)
            link(nc.vector.tensor_tensor(rel_near[:, :].rearrange("p (w t) -> p w t", t=WIN_TILES),
                                         dst_f[:, :].rearrange("p (w t) -> p w t", t=WIN_TILES),
                                         small[:, 0:WINS].rearrange("p (w o) -> p w o", o=1)
                                         .broadcast_to((P, WINS, WIN_TILES)), ALU.subtract))
            link(nc.vector.tensor_copy(row_near[:, :], small[0:1, 0:WINS]))
            link(nc.vector.tensor_scalar(outside[:, :], rel_near[:, :], 0.0, None, ALU.is_lt))
            link(nc.vector.tensor_scalar(above[:, :], rel_near[:, :], float(WIN - 1), None, ALU.is_gt))
            link(nc.vector.tensor_tensor(outside[:, :], outside[:, :], above[:, :], ALU.add))
            nc.vector.reduce_sum(outside_n[:, :], outside[:, :], AX).then_inc(s_outside, 1)
            dve.wait_ge(s_outside, 1)
            for rel in (rel_near, rel_far):
                if rel is rel_far:
                    link(nc.vector.tensor_copy(rel_far[:, :], dst_f[:, :]))
                link(nc.vector.memset(rel[0:P, FULL_TILES + 1:TILES], -1e5))
                link(nc.vector.tensor_tensor(rel[:, FULL_TILES:FULL_TILES + 1], rel[:, FULL_TILES:FULL_TILES + 1],
                                             elem[:, 1:2], ALU.add))
            dve.wait_ge(s_idx, 16 * 5)
            link(nc.vector.tensor_scalar(off_a[:, :], paths_sb[:, :, 0], float(EXT), None, ALU.mult))
            link(nc.vector.tensor_scalar(packed_f[:, :], paths_sb[:, :, 1], float(EXT * 65536), None, ALU.mult))
            link(nc.vector.tensor_tensor(packed_f[:, :], packed_f[:, :], off_a[:, :], ALU.add))
            link(nc.vector.tensor_copy(packed[:, :], packed_f[:, :]))
            link(nc.vector.tensor_scalar(i3_col[:, :], i3_sb[:, :], float(EIGHTH), elem[:, 0:1], ALU.mult, ALU.add))
            for c in range(CHUNKS):
                last = nc.vector.tensor_scalar(combine[:, c, :], cols[:, :], i3_col[:, c:c + 1], coef_sb[:, c:c + 1],
                                               ALU.is_equal, ALU.mult)
            last.then_inc(s_combine, 1)
            dve.wait_ge(s_outside_sum, 1)
            link(nc.vector.tensor_copy(far_flag[:, :], small[0:1, 64:65]))
            nc.vector.tensor_copy(ident_b[:, :], ident[:, :]).then_inc(s_ready, 1)

            dve.wait_ge(s_weight, 16)
            nc.vector.tensor_reduce(mx[:, 1:2], w_sb.rearrange("p a b -> p (a b)"), AX, ALU.max,
                                    apply_absolute_value=True).then_inc(s_wmax, 1)
            dve.wait_ge(s_mxT, 1)
            nc.vector.reduce_max(mx_all[:, 1:2], small[0:1, 128:256], AX).then_inc(s_mx1, 1)
            dve.wait_ge(s_mxb, 1)
            fp8_scale(1)
            link(to_fp8(w_sb, w_tmp, w_exp, wq[:, :, :], 1))
            nc.vector.engine_nop().then_inc(s_wmax, 1)

            regs = [dve.alloc_register(f"path_{p}") for p in range(PATHS // 2)]
            ra, rb = dve.alloc_register("off_a"), dve.alloc_register("off_b")

            def windows(rel, g, b):
                nc.vector.tensor_tensor(
                    onehot[b][:, :, :],
                    rel[:, bass.ds(g * GROUP_TILES, GROUP_TILES)].rearrange("p (t o) -> p t o", o=1)
                    .broadcast_to((P, GROUP_TILES, WIN)),
                    cols[:, 0:WIN].rearrange("p (o n) -> p o n", o=1).broadcast_to((P, GROUP_TILES, WIN)),
                    ALU.is_equal).then_inc(s_onehot[b], 1)

            def load_paths(c):
                for h in range(2):
                    dve.load(regs[16 * h:16 * h + 16], packed[0:1, c * CHUNK + 16 * h:c * CHUNK + 16 * h + 16])

            def edge_pass(n, rel):
                with dve.Fori(0, PAIRS) as it:
                    k = n * PAIRS + it
                    for b in range(2):
                        load_paths(0)
                        dve.wait_ge(s_x1[b], k * (16 * GROUP_TILES) + 16 * GROUP_TILES)
                        dve.wait_ge(s_x2[b], k * 32 + 32)
                        for c in range(CHUNKS):
                            s = c % 2
                            dve.wait_ge(s_scattered[s], AHEAD + k * CHUNKS + (2 * b + c // 2))
                            if c == 0:
                                windows(rel, 2 * it + b, b)
                            for q in range(CHUNK):
                                r = regs[(c % 2) * CHUNK + q]
                                dve.reg_alu(ra, r, 0xFFFF, ALU.bitwise_and)
                                dve.reg_alu(rb, r, 16, ALU.logical_shift_right)
                                a = dve.snap(ra, min_val=0, max_val=DIM - EXT)
                                bb = dve.snap(rb, min_val=0, max_val=DIM - EXT)
                                last = nc.vector.tensor_tensor(prod[s][:, :, q, :], x1[b][:, :, bass.ds(a, EXT)],
                                                               x2[b][:, :, bass.ds(bb, EXT)], ALU.mult)
                            last.then_inc(s_prod[s], 1)
                            if c == 1:
                                load_paths(2)

            def far(p):
                dve.wait_ge(s_far, p * 3 + 2)
                dve.sem_inc(s_waited_dve, 1)
                edge_pass(p, rel_far)

            branch_on(dve, lambda: edge_pass(0, rel_near), far)

            nc.vector.memset(nodes1[96:P, NT - 1, :], 0.0).then_inc(s_zrow, 1)
            dve.wait_ge(s_back, 16 * 2 * QUARTERS)
            for t in range(NT):
                layer_stats(nodes1, t)
            rstd_of(2)
            for t in range(NT):
                link(nc.vector.tensor_scalar(y[:, t, :], nodes1[:, t, :], mv[:, t, 0:1], rstd[:, t:t + 1],
                                             ALU.subtract, ALU.mult))
            nc.vector.tensor_reduce(mx[:, 0:1], y.rearrange("p a b -> p (a b)"), AX, ALU.max,
                                    apply_absolute_value=True).then_inc(s_wmax, 1)
            dve.wait_ge(s_mxT, 2)
            nc.vector.reduce_max(mx_all[:, 0:1], small[0:1, 128:256], AX).then_inc(s_mx1, 1)
            dve.wait_ge(s_mxb, 2)
            fp8_scale(0)
            link(nc.vector.tensor_tensor(out_scale[:, :], scale_inv[:, 0:1], scale_inv[:, 1:2], ALU.mult))
            for t in range(NT):
                to_fp8(y[:, t, :], y[:, t, :], tmp[:, t, :], yq[:, t, :], 0).then_inc(s_yq, 1)
            for t in range(NT):
                dve.wait_ge(s_mm, t + 1)
                nc.vector.scalar_tensor_tensor(
                    out=res[:, t, :], in0=comb[t % 2][:, :, :].rearrange("p a b -> p (a b)"),
                    scalar=out_scale[:, 0:1], in1=nodes1[:, t, :],
                    op0=ALU.mult, op1=ALU.add).then_inc(s_res, 1)

        @block.scalar
        def _(act):
            act.dma_start(src_sb[:, :], src_t).then_inc(s_idx, 16)
            act.dma_start(dst_sb[:, :], dst_t).then_inc(s_idx, 16)
            act.dma_start(ident[:, :], ident_c).then_inc(s_const, 16)
            act.dma_start(cols[:, :], cols_c).then_inc(s_const, 16)
            act.dma_start(elem[:, :], elem_c).then_inc(s_const, 16)
            act.wait_ge(s_idx, 32)
            act.dma_start(paths_sb[:, :, :], paths.rearrange("(o p) k -> o p k", o=1)).then_inc(s_idx, 16)
            act.dma_start(i3_sb[:, :], i3_rep).then_inc(s_idx, 16)
            act.dma_start(coef_sb[:, :], coef_rep).then_inc(s_idx, 16)
            act.dma_start(w_sb, weight_q.rearrange("q k n -> k q n")).then_inc(s_weight, 16)
            act.wait_ge(s_var, 1)
            nc.scalar.activation(std[:, :], var_e[:, :], ACT.Sqrt).then_inc(s_std, 1)
            act.wait_ge(s_normed, 1)
            act.dma_start(xn_dram[0:(NT - 1) * P, :].rearrange("(t p) c -> p t c", p=P),
                          normed0[:, 0:NT - 1, :]).then_inc(s_normed_out, 16)
            act.dma_start(xn_dram[(NT - 1) * P:NODES, :], normed0[0:LAST, NT - 1, :]).then_inc(s_normed_out, 16)
            act.wait_ge(s_ready, 1)
            for ahead in (*s_sums, *s_sums_T, *s_rows):
                act.sem_inc(ahead, AHEAD)

            def edge_pass(n):
                with act.Fori(0, PAIRS) as it:
                    k = n * PAIRS + it
                    for c in range(BODY_CHUNKS + 1):
                        s = c % 2
                        if c >= 1:
                            act.wait_ge(s_turned[1 - s], k * CHUNKS + ((c - 1) // 2 + 1))
                            nc.scalar.activation(sums_T[1 - s][:, :, :], turn[1 - s][:, :, :], ACT.Copy)\
                                .then_inc(s_sums_T[1 - s], 1)
                        if c < BODY_CHUNKS:
                            act.wait_ge(s_scattered[s], AHEAD + k * CHUNKS + (c // 2 + 1))
                            nc.scalar.activation(sums[s][:, :, :], acc[s][:, :, :], ACT.Copy).then_inc(s_sums[s], 1)
                        if c in (CHUNKS, 2 * CHUNKS):
                            b = c // CHUNKS - 1
                            act.wait_ge(s_combined[b], k + 1)
                            act.wait_ge(s_rows_free[b], AHEAD + k)
                            nc.scalar.activation(rows[b][:, :, :], comb[b][:, :, :], ACT.Copy).then_inc(s_rows[b], 1)

            branch_on(act, lambda: edge_pass(0), edge_pass)

            act.wait_ge(s_var, 2)
            nc.scalar.activation(std[:, :], var_e[:, :], ACT.Sqrt).then_inc(s_std, 1)
            for t in range(NT):
                act.wait_ge(s_yT, t + 1)
                nc.scalar.activation(yqT[:, t, :, :], turn_b[t % 2], ACT.Copy).then_inc(s_yTc, 1)

        @block.tensor
        def _(pe):
            for s in range(2):
                pe.sem_inc(s_scattered[s], AHEAD)
            pe.wait_ge(s_dstf, 1)
            nc.tensor.matmul(small[:, 0:WINS], ones[0:1, :], dst_f[0:1, 0:TILES:WIN_TILES], start=True, stop=True)\
                .then_inc(s_base, 1)
            pe.wait_ge(s_outside, 1)
            nc.tensor.matmul(small[0:1, 64:65], outside_n[:, :], ones[:, 0:1], start=True, stop=True)\
                .then_inc(s_outside_sum, 1)
            pe.wait_ge(s_const, 16 * 3)

            def spread_max(k, n):
                pe.wait_ge(s_wmax, n)
                nc.tensor.transpose(small[0:1, 128:256], mx[:, k:k + 1], ident[:, :]).then_inc(s_mxT, 1)
                pe.wait_ge(s_mx1, 2 - k)
                nc.tensor.matmul(small[:, k:k + 1], ones[0:1, :], mx_all[0:1, k:k + 1], start=True, stop=True)\
                    .then_inc(s_mxb, 1)

            pe.wait_ge(s_ready, 1)
            spread_max(1, 1)
            pe.wait_ge(s_combine, 1)

            def scatter(k, b, c):
                s = c % 2
                if c == 0:
                    pe.wait_ge(s_onehot[b], k + 1)
                pe.wait_ge(s_prod[s], AHEAD + k * CHUNKS + (2 * b + c // 2 + 1))
                pe.wait_ge(s_sums[s], AHEAD + k * CHUNKS + (2 * b + c // 2))
                for t in range(GROUP_TILES):
                    for q in range(QUARTERS):
                        last = nc.tensor.matmul(acc[s][32 * q:32 * q + 32, t // WIN_TILES, :], onehot[b][:, t, :],
                                                prod[s][:, t, :, EIGHTH * q:EIGHTH * q + EIGHTH],
                                                start=(t == 0), stop=(t == GROUP_TILES - 1),
                                                skip_group_check=True)
                last.then_inc(s_scattered[s], 1)

            def turn_chunk(k, c):
                s = c % 2
                pe.wait_ge(s_sums[s], AHEAD + k * CHUNKS + (c // 2 + 1))
                pe.wait_ge(s_sums_T[s], AHEAD + k * CHUNKS + c // 2)
                for w in range(GROUP_WINS):
                    last = nc.tensor.transpose(turn[s][:, w, :], sums[s][:, w, :], ident[:, :])
                last.then_inc(s_turned[s], 1)

            def combine_chunk(k, c):
                s, b, cc = c % 2, c // CHUNKS, c % CHUNKS
                pe.wait_ge(s_sums_T[s], AHEAD + k * CHUNKS + (c // 2 + 1))
                if cc == 0:
                    pe.wait_ge(s_rows[b], AHEAD + k)
                for w in range(GROUP_WINS):
                    last = nc.tensor.matmul(comb[b][:, w, :], sums_T[s][:, w, :], combine[:, cc, :],
                                            start=(cc == 0 and w == 0), stop=(cc == CHUNKS - 1),
                                            skip_group_check=True)
                if cc == CHUNKS - 1:
                    last.then_inc(s_combined[b], 1)

            def edge_pass(n):
                with pe.Fori(0, PAIRS) as it:
                    k = n * PAIRS + it
                    for c in range(BODY_CHUNKS + 1):
                        if c >= 1:
                            turn_chunk(k, c - 1)
                        if c < BODY_CHUNKS:
                            scatter(k, c // CHUNKS, c % CHUNKS)
                        if c >= 1:
                            combine_chunk(k, c - 1)

            branch_on(pe, lambda: edge_pass(0), edge_pass)

            spread_max(0, 3)
            for t in range(NT + 1):
                if t < NT:
                    pe.wait_ge(s_yq, t + 1)
                    if t >= 2:
                        pe.wait_ge(s_yTc, t - 1)
                    for q in range(QUARTERS):
                        last = nc.tensor.transpose(turn_b[t % 2][:, q, :], yq[:, t, q * P:(q + 1) * P], ident_b[:, :])
                    last.then_inc(s_yT, 1)
                if t >= 1:
                    pe.wait_ge(s_yTc, t)
                    if t >= 3:
                        pe.wait_ge(s_res, t - 2)
                    for q in range(QUARTERS):
                        last = nc.tensor.matmul(comb[(t - 1) % 2][:, :, :], yqT[:, t - 1, q, :], wq[:, q, :],
                                                start=(q == 0), stop=(q == QUARTERS - 1))
                    last.then_inc(s_mm, 1)


def kernel(x, src, dst, edge_attr_512, L0_gnn_path_coeffs, L0_gnn_path_indices, L0_ffn_weight):
    import numpy as np
    import concourse.bacc as bacc
    from concourse.bass_utils import run_bass_kernel_spmd

    x, src, dst, edges, coef, paths, weight = (np.asarray(a) for a in (
        x, src, dst, edge_attr_512, L0_gnn_path_coeffs, L0_gnn_path_indices, L0_ffn_weight))
    order = np.concatenate([np.arange(FULL_TILES * P)] + [np.arange(EDGES - P, EDGES)] * 2)
    elem = np.stack([np.arange(P) % EIGHTH, np.where(np.arange(P) < P - TAIL, -1e5, 0.0)], 1)
    arrays = {
        "x": x,
        "x_quarters": x.reshape(NODES, SEGS, QUARTERS, EIGHTH).transpose(2, 0, 1, 3).reshape(QUARTERS, NODES, QCOLS),
        "edges": edges,
        "src_t": src[order].reshape(TILES, P).T,
        "dst_t": dst[order].reshape(TILES, P).T,
        "paths": paths,
        "i3_rep": np.repeat(paths[:, 2].reshape(CHUNKS, CHUNK), EIGHTH, 1).T,
        "coef_rep": np.repeat(coef.reshape(CHUNKS, CHUNK), EIGHTH, 1).T,
        "weight_q": weight.reshape(SEGS, QUARTERS, EIGHTH, SEGS, QUARTERS, EIGHTH).transpose(1, 0, 2, 4, 3, 5)
        .reshape(QUARTERS, P, DIM),
        "ident_c": np.eye(P, dtype=np.float32),
        "cols_c": np.tile(np.arange(P, dtype=np.float32), (P, 1)),
        "elem_c": elem.astype(np.float32),
    }
    nc = bacc.Bacc("TRN2", target_bir_lowering=False, num_devices=1)
    arrays = {k: np.ascontiguousarray(a) for k, a in arrays.items()}
    aps = {k: nc.dram_tensor(k, a.shape, mybir.dt.from_np(a.dtype), kind="ExternalInput").ap()
           for k, a in arrays.items()}
    out = nc.dram_tensor("out", (NODES, DIM), mybir.dt.float32, kind="ExternalOutput").ap()
    gnn_ffn(nc, **aps, out=out)
    r = run_bass_kernel_spmd(nc, [arrays], core_ids=[0])
    return np.ascontiguousarray(r.results[0]["out"].reshape(NODES, QUARTERS, SEGS, EIGHTH).transpose(0, 2, 1, 3)
                                .reshape(NODES, DIM))
```

```python
import concourse.bass as bass
from concourse import mybir
from concourse.alu_op_type import AluOpType as ALU
from contextlib import ExitStack

NODES, EDGES, DIM, PATHS = 1250, 21250, 512, 64
SEGS, EXT = 16, 32
P = 128
QUARTERS, EIGHTH = 4, 8
QCOLS = SEGS * EIGHTH
WIN = 32
WIN_TILES, GROUP_TILES = 3, 12
GROUP_WINS = GROUP_TILES // WIN_TILES
FULL_TILES = EDGES // P
TAIL = EDGES - FULL_TILES * P
GROUPS = -(-(FULL_TILES + 1) // GROUP_TILES)
TILES = GROUPS * GROUP_TILES
WINS = TILES // WIN_TILES
PAIRS = GROUPS // 2
MAIN_TILES = 10
CHUNK = 16
CHUNKS = PATHS // CHUNK
BODY_CHUNKS = 2 * CHUNKS
AHEAD = 1
GEN_PASSES = -(-NODES // WIN)
TABLE_ROWS = NODES + WIN
NT = 10
LAST = NODES - (NT - 1) * P
HALF = NT // 2
X_CUTS = [(0, 3), (3, HALF), (HALF, 8), (8, NT)]
EARLY = NT - 1
LAST_WINS = WINS - GROUP_WINS
ORDERED = WINS - 2
CHECKS = TILES + ORDERED + GROUP_WINS
PAIR = 2
NPAIRS = NT // PAIR
FP8_MAX = 448.0
F32_ROUND = 1.5 * 2.0 ** 20


def gnn_ffn(nc, x, x_quarters, edges, src_t, dst_t, paths, i3_rep, coef_rep, weight_q,
            ident_c, cols_c, elem_c, out):
    fp32, bf16, i32 = mybir.dt.float32, mybir.dt.bfloat16, mybir.dt.int32
    ACT = mybir.ActivationFunctionType
    AX = mybir.AxisListType.X

    ctx = ExitStack()
    with ctx:
        def sb(name, shape, dt=fp32):
            return ctx.enter_context(nc.sbuf_tensor(name, shape, dt))

        def pb(name, shape, dt=fp32):
            return ctx.enter_context(nc.psum_tensor(name, shape, dt))

        def sem(name):
            return ctx.enter_context(nc.semaphore(name))

        xn_dram = nc.dram_tensor("xn_dram", [NODES, DIM], fp32, kind="Internal").ap()
        table = nc.dram_tensor("sum_table", [QUARTERS, TABLE_ROWS, QCOLS], fp32, kind="Internal").ap()

        x1 = [sb(f"x1_{b}", [P, GROUP_TILES, DIM]) for b in range(2)]
        x2 = [sb(f"x2_{b}", [P, GROUP_TILES, DIM]) for b in range(2)]
        prod = [sb(f"prod_{s}", [P, GROUP_TILES, CHUNK, EXT]) for s in range(2)]
        onehot = [sb(f"onehot_{b}", [P, GROUP_TILES, WIN]) for b in range(2)]
        src_slot = [sb(f"src_slot_{b}", [P, GROUP_TILES], i32) for b in range(2)]
        sums = [sb(f"sums_{s}", [P, GROUP_WINS, CHUNK * EIGHTH]) for s in range(2)]
        sums_T = [sb(f"sums_T_{s}", [P, GROUP_WINS, P]) for s in range(2)]
        rows = [sb(f"rows_{b}", [P, GROUP_WINS, QCOLS]) for b in range(2)]
        src_sb = sb("src_sb", [P, TILES], i32)
        dst_sb = sb("dst_sb", [P, TILES], i32)
        dst_f = sb("dst_f", [P, TILES])
        rel_near = sb("rel_near", [P, TILES])
        rel_far = sb("rel_far", [P, TILES])
        base_f = sb("base_f", [P, WINS])
        outside = sb("outside", [P, CHECKS])
        above = sb("above", [P, TILES])
        outside_n = sb("outside_n", [P, 1])
        far_flag = sb("far_flag", [1, 1], i32)
        row_near = sb("row_near", [1, WINS], i32)
        row_far_f = sb("row_far_f", [1, WINS])
        row_far = sb("row_far", [1, WINS], i32)
        paths_sb = sb("paths_sb", [1, PATHS, 3], i32)
        off_a = sb("off_a", [1, PATHS])
        packed_f = sb("packed_f", [1, PATHS])
        packed = sb("packed", [1, PATHS], i32)
        i3_sb = sb("i3_sb", [P, CHUNKS], i32)
        coef_sb = sb("coef_sb", [P, CHUNKS])
        i3_col = sb("i3_col", [P, CHUNKS])
        combine = sb("combine", [P, CHUNKS, QCOLS])
        ident = sb("ident", [P, P])
        ident_b = sb("ident_b", [P, P], bf16)
        cols = sb("cols", [P, P])
        elem = sb("elem", [P, 2])
        ones = sb("ones", [P, P])
        zeros = sb("zeros", [P, QCOLS])
        stats = sb("stats", [P, NT, 6])
        mv = sb("mv", [P, NT, 2])
        var_e = sb("var_e", [P, NT])
        std = sb("std", [P, NT])
        inv = sb("inv", [P, NT])
        quot = sb("quot", [P, NT])
        rstd = sb("rstd", [P, NT])
        wq = sb("wq", [P, QUARTERS, DIM], bf16)
        mx = sb("mx", [P, 2])
        mx_tile = sb("mx_tile", [P, NT])
        shift = sb("shift", [P, NT])
        mx_all = sb("mx_all", [1, 2])
        mx_bc = sb("mx_bc", [P, 2])
        mx_inv = sb("mx_inv", [P, 2])
        scale = sb("scale", [P, 2])
        scale_inv = sb("scale_inv", [P, 2])
        out_scale = sb("out_scale", [P, 1])
        nodes0 = prod[0][:, :, :, :].rearrange("p t q e -> p (t q e)")[:, 0:NT * DIM]\
            .rearrange("p (t c) -> p t c", c=DIM)
        normed0 = prod[1][:, :, :, :].rearrange("p t q e -> p (t q e)")[:, 0:NT * DIM]\
            .rearrange("p (t c) -> p t c", c=DIM)
        w_sb, w_tmp, w_exp = (sb(name, [P, QUARTERS, DIM])[:, :, :] for name in ("w_sb", "w_tmp", "w_exp"))
        nodes1 = x1[0][:, 0:NT, :]
        y = x2[0][:, 0:NT, :]
        expo = x2[1][:, 0:NT, :]
        yq = prod[0][:, :, :, :].rearrange("p t q e -> p (t q e)")[:, 0:NT * DIM // 2]\
            .bitcast(bf16).rearrange("p (t c) -> p t c", c=DIM)
        yqT = prod[0][:, :, :, :].rearrange("p t q e -> p (t q e)")[:, NT * DIM // 2:NT * DIM]\
            .bitcast(bf16).rearrange("p (t k c) -> p t k c", k=4, c=P)
        res = normed0

        acc = [pb(f"acc_{s}", [P, GROUP_WINS, CHUNK * EIGHTH]) for s in range(2)]
        turn = [pb(f"turn_{s}", [P, GROUP_WINS, P]) for s in range(2)]
        comb = [pb(f"comb_{b}", [P, GROUP_WINS, QCOLS]) for b in range(2)]
        small = pb("small", [P, 512])
        turn_b = [turn[s][:, :, :].rearrange("p w c -> p (w c)").bitcast(bf16)
                  .rearrange("p (t q c) -> p t q c", t=PAIR, q=QUARTERS) for s in range(2)]
        ffn_out = [t[:, :, :].rearrange("p a b -> p (a b)") for t in (*comb, *acc)]

        s_const = sem("s_const")
        s_nodes = [sem(f"s_nodes_{i}") for i in range(len(X_CUTS))]
        s_dst = sem("s_dst")
        s_src_in = sem("s_src_in")
        s_paths = sem("s_paths")
        s_weight = sem("s_weight")
        s_init = sem("s_init")
        s_dve = sem("s_dve")
        s_var = sem("s_var")
        s_std = sem("s_std")
        s_normed = sem("s_normed")
        s_normed_out = sem("s_normed_out")
        s_dstf = sem("s_dstf")
        s_base = sem("s_base")
        s_outside = sem("s_outside")
        s_outside_sum = sem("s_outside_sum")
        s_flag = sem("s_flag")
        s_ready = sem("s_ready")
        s_combine = sem("s_combine")
        s_table_init = sem("s_table_init")
        s_zero = sem("s_zero")
        s_x1 = [sem(f"s_x1_{b}") for b in range(2)]
        s_x2 = [sem(f"s_x2_{b}") for b in range(2)]
        s_src = sem("s_src")
        s_onehot = [sem(f"s_onehot_{b}") for b in range(2)]
        s_prod = [sem(f"s_prod_{s}") for s in range(2)]
        s_scattered = [sem(f"s_scattered_{s}") for s in range(2)]
        s_sums = [sem(f"s_sums_{s}") for s in range(2)]
        s_turned = [sem(f"s_turned_{s}") for s in range(2)]
        s_sums_T = [sem(f"s_sums_T_{s}") for s in range(2)]
        s_combined = [sem(f"s_combined_{b}") for b in range(2)]
        s_rows = [sem(f"s_rows_{b}") for b in range(2)]
        s_added = [sem(f"s_added_{b}") for b in range(2)]
        s_rows_free = [sem(f"s_rows_free_{b}") for b in range(2)]
        s_far = sem("s_far")
        s_waited_pool = sem("s_waited_pool")
        s_waited_dve = sem("s_waited_dve")
        s_waited_sp = sem("s_waited_sp")
        s_table_done = sem("s_table_done")
        s_back = [sem(f"s_back_{h}") for h in range(2)]
        s_zrow = sem("s_zrow")
        s_wmax = sem("s_wmax")
        s_mxT = sem("s_mxT")
        s_mx1 = sem("s_mx1")
        s_mxb = sem("s_mxb")
        s_norm = sem("s_norm")
        s_y = sem("s_y")
        s_xscale = sem("s_xscale")
        s_v = sem("s_v")
        s_expo = sem("s_expo")
        s_magic = sem("s_magic")
        s_yq = sem("s_yq")
        s_yT = sem("s_yT")
        s_yTc = sem("s_yTc")
        s_mm = sem("s_mm")
        s_res = sem("s_res")
        s_out = sem("s_out")

        block = ctx.enter_context(nc.Block())

        def branch_on(eng, near, far):
            flag = eng.alloc_register("flag")
            eng.load(flag, far_flag[0:1, 0:1])
            with eng.If_eq(flag, 0):
                near()
            with eng.Else():
                with eng.Fori(0, GEN_PASSES) as p:
                    far(p)
            eng.nop()

        @block.sync
        def _(sp):
            sp.dma_start(dst_sb[:, :], dst_t).then_inc(s_dst, 16)
            for i, (t0, t1) in enumerate(X_CUTS):
                full = min(t1, NT - 1)
                sp.dma_start(nodes0[:, t0:full, :],
                             x[t0 * P:full * P, :].rearrange("(t p) c -> p t c", p=P)).then_inc(s_nodes[i], 16)
            sp.wait_ge(s_zrow, 1)
            sp.dma_start(nodes0[0:LAST, NT - 1, :], x[(NT - 1) * P:NODES, :]).then_inc(s_nodes[-1], 16)

            def load(g, b, tail=False):
                row = g * (GROUP_TILES * P)
                sp.dma_start(x2[b][:, 0:MAIN_TILES, :],
                             edges[bass.ds(row, MAIN_TILES * P), :].rearrange("(t p) c -> p t c", p=P))\
                    .then_inc(s_x2[b], 16)
                if not tail:
                    sp.dma_start(x2[b][:, MAIN_TILES:GROUP_TILES, :],
                                 edges[bass.ds(row + MAIN_TILES * P, 2 * P), :]
                                 .rearrange("(t p) c -> p t c", p=P)).then_inc(s_x2[b], 16)
                else:
                    sp.dma_start(x2[b][:, MAIN_TILES:GROUP_TILES, :],
                                 edges[EDGES - P:EDGES, :].rearrange("(o p) c -> p o c", o=1)
                                 .broadcast_to((P, 2, DIM))).then_inc(s_x2[b], 16)

            def edge_pass(n):
                sp.wait_ge(s_prod[1], n * (PAIRS * CHUNKS) + AHEAD)
                load(0, 0)
                sp.wait_ge(s_x1[0], n * (16 * PAIRS * GROUP_TILES) + 16 * GROUP_TILES)
                load(1, 1)

                def step(it):
                    for b in range(2):
                        sp.wait_ge(s_prod[1], AHEAD + (n * PAIRS + it) * CHUNKS + (2 * b - 2))
                        load(2 * it + b, b)
                with sp.Fori(1, PAIRS - 1) as it:
                    step(it)
                for b in range(2):
                    sp.wait_ge(s_prod[1], AHEAD + (n * PAIRS + PAIRS - 1) * CHUNKS + (2 * b - 2))
                    load(GROUPS - 2 + b, b, tail=(b == 1))

            def far(p):
                edge_pass(p)
                sp.wait_ge(s_rows_free[1], AHEAD + (p + 1) * PAIRS)
                sp.sem_inc(s_waited_sp, 1)

            def near():
                edge_pass(0)
                sp.wait_ge(s_prod[1], AHEAD + (PAIRS - 1) * CHUNKS + CHUNKS // 2)
                sp.wait_ge(s_rows_free[0], AHEAD + PAIRS)
                sp.wait_ge(s_rows_free[1], AHEAD + PAIRS - 1)

            sp.wait_ge(s_flag, 1)
            branch_on(sp, near, far)

            for q in range(QUARTERS):
                sp.dma_start(nodes1[:, 0:EARLY, q * QCOLS:(q + 1) * QCOLS],
                             table[q, 0:EARLY * P, :].rearrange("(t p) c -> p t c", p=P)).then_inc(s_back[0], 16)
            sp.wait_ge(s_table_done, 1)
            sp.wait_ge(s_zrow, 2)
            sp.dma_start(nodes1[0:LAST, NT - 1, :].rearrange("p (q c) -> p q c", q=QUARTERS),
                         table[:, EARLY * P:NODES, :].rearrange("q p c -> p q c")).then_inc(s_back[1], 16)
            for t in range(NT):
                sp.wait_ge(s_res, t + 1)
                n = P if t < NT - 1 else LAST
                sp.dma_start(out[t * P:t * P + n, :], res[0:n, t, :]).then_inc(s_out, 16)
            sp.wait_ge(s_out, 16 * NT)

        @block.gpsimd
        def _(pool):
            def take_wait():
                pool.sem_inc(s_waited_pool, 1)

            def indices(g, b):
                nc.gpsimd.tensor_copy(src_slot[b][:, :], src_sb[:, bass.ds(g * GROUP_TILES, GROUP_TILES)])\
                    .then_inc(s_src, 1)

            def gather(n, it, b):
                pool.wait_ge(s_src, (n * PAIRS + it) * 2 + (b + 1))
                take_wait()
                for t in range(GROUP_TILES):
                    nc.gpsimd.indirect_dma_start(
                        out=x1[b][:, t, :], out_offset=None, in_=xn_dram,
                        in_offset=bass.IndirectOffsetOnAxis(ap=src_slot[b][:, t:t + 1], axis=0))\
                        .then_inc(s_x1[b], 16)

            def add_rows(n, it, b, row_of, regs, steps):
                pool.load(regs, row_of[0:1, bass.ds((2 * it + b) * GROUP_WINS, GROUP_WINS)])
                k = n * PAIRS + it
                pool.wait_ge(s_table_init, 16 * (1 + QUARTERS))
                pool.wait_ge(s_rows[b], AHEAD + k + 1)
                done = 0
                for step in steps:
                    for w in step:
                        row = pool.snap(regs[w], min_val=0, max_val=TABLE_ROWS - WIN)
                        pool.dma_start(table[:, bass.ds(row, WIN), :], rows[b][:, w, :], accum_op=ALU.add)\
                            .then_inc(s_added[b], 16)
                    done += len(step)
                    pool.wait_ge(s_added[b], k * (16 * GROUP_WINS) + 16 * done)
                    if done < GROUP_WINS:
                        take_wait()
                pool.sem_inc(s_rows_free[b], 1)

            def edge_pass(n, row_of, regs, steps):
                for b in range(2):
                    indices(b, b)
                    gather(n, 0, b)
                with pool.Fori(1, PAIRS) as it:
                    for b in range(2):
                        k = n * PAIRS + it
                        pool.wait_ge(s_prod[1], AHEAD + k * CHUNKS + (2 * b - 2))
                        take_wait()
                        indices(2 * it + b, b)
                        gather(n, it, b)
                        add_rows(n, it - 1, b, row_of, regs, steps)
                for b in range(2):
                    add_rows(n, PAIRS - 1, b, row_of, regs, steps)

            for b in range(2):
                pool.sem_inc(s_rows_free[b], AHEAD)
            nc.gpsimd.memset(zeros[:, :], 0.0).then_inc(s_zero, 1)
            nc.gpsimd.memset(row_far_f[:, :], 0.0).then_inc(s_far, 1)
            pool.wait_ge(s_far, 1)
            nc.gpsimd.tensor_copy(row_far[:, :], row_far_f[:, :]).then_inc(s_far, 1)
            pool.wait_ge(s_src_in, 16)
            pool.wait_ge(s_flag, 1)
            pool.wait_ge(s_far, 2)
            pool.wait_ge(s_normed_out, 16 * 3)
            regs = [pool.alloc_register(f"row_{w}") for w in range(GROUP_WINS)]

            def near():
                edge_pass(0, row_near, regs, steps=((0, 2), (1, 3)))

            def far(p):
                pool.wait_ge(s_ready, 1)
                edge_pass(p, row_far, regs, steps=((0,), (1,), (2,), (3,)))
                nc.gpsimd.tensor_scalar(rel_far[:, :], rel_far[:, :], float(-WIN), None, ALU.add).then_inc(s_far, 1)
                nc.gpsimd.tensor_scalar(row_far_f[:, :], row_far_f[:, :], float(WIN), None, ALU.add)\
                    .then_inc(s_far, 1)
                pool.wait_ge(s_far, p * 3 + 4)
                take_wait()
                nc.gpsimd.tensor_copy(row_far[:, :], row_far_f[:, :]).then_inc(s_far, 1)
                pool.wait_ge(s_far, p * 3 + 5)

            branch_on(pool, near, far)
            pool.nop().then_inc(s_table_done, 1)

        @block.vector
        def _(dve):
            chain = [0]

            def link(ins):
                chain[0] += 1
                ins.then_inc(s_dve, 1)
                dve.wait_ge(s_dve, chain[0])

            def layer_stats(nodes, t0, t1, landed=()):
                tiles = range(t0, t1)
                first = chain[0]
                for t in tiles:
                    if t in landed:
                        dve.wait_ge(*landed[t])
                    chain[0] += 1
                    nc.vector.bn_stats(stats[:, t, :], nodes[:, t, :]).then_inc(s_dve, 1)
                for i, t in enumerate(tiles):
                    dve.wait_ge(s_dve, first + i + 1)
                    chain[0] += 1
                    nc.vector.bn_aggr(mv[:, t, :], stats[:, t, :]).then_inc(s_dve, 1)
                dve.wait_ge(s_dve, chain[0])
                nc.vector.tensor_scalar(var_e[:, t0:t1], mv[:, t0:t1, 1], 1e-5, None, ALU.add).then_inc(s_var, 1)

            def rstd_of(t0, t1, k):
                cs = slice(t0, t1)
                dve.wait_ge(s_std, k)
                link(nc.vector.reciprocal(inv[:, cs], std[:, cs]))
                link(nc.vector.tensor_tensor(quot[:, cs], var_e[:, cs], inv[:, cs], ALU.mult))
                link(nc.vector.tensor_tensor(quot[:, cs], quot[:, cs], std[:, cs], ALU.add))
                link(nc.vector.tensor_scalar(quot[:, cs], quot[:, cs], 0.5, None, ALU.mult))
                link(nc.vector.reciprocal(rstd[:, cs], quot[:, cs]))

            def fp8_scale(k):
                link(nc.vector.tensor_scalar(mx_bc[:, k:k + 1], small[:, k:k + 1], 1e-12, None, ALU.max))
                link(nc.vector.reciprocal(mx_inv[:, k:k + 1], mx_bc[:, k:k + 1]))
                link(nc.vector.tensor_scalar(scale[:, k:k + 1], mx_inv[:, k:k + 1], FP8_MAX, None, ALU.mult))
                link(nc.vector.reciprocal(scale_inv[:, k:k + 1], scale[:, k:k + 1]))

            def weight_to_fp8():
                link(nc.vector.tensor_scalar(w_tmp, w_sb, scale[:, 1:2], FP8_MAX, ALU.mult, ALU.min))
                link(nc.vector.tensor_scalar(w_tmp, w_tmp, -FP8_MAX, None, ALU.max))
                link(nc.vector.tensor_scalar(w_exp.bitcast(i32), w_tmp.bitcast(i32), 0x7F800000, None,
                                             ALU.bitwise_and))
                link(nc.vector.tensor_scalar(w_exp, w_exp, 2.0 ** -6, F32_ROUND, ALU.max, ALU.mult))
                link(nc.vector.tensor_tensor(w_tmp, w_tmp, w_exp, ALU.add))
                nc.vector.tensor_tensor(wq[:, :, :], w_tmp, w_exp, ALU.subtract).then_inc(s_wmax, 1)

            for s in range(2):
                dve.sem_inc(s_prod[s], AHEAD)
            nc.vector.memset(nodes0[96:P, NT - 1, :], 0.0).then_inc(s_zrow, 1)
            link(nc.vector.memset(ones[:, :], 1.0))
            dve.wait_ge(s_dst, 16)
            nc.vector.tensor_copy(dst_f[:, :], dst_sb[:, :]).then_inc(s_dstf, 1)
            dve.wait_ge(s_base, 1)
            link(nc.vector.tensor_tensor(rel_near[:, :].rearrange("p (w t) -> p w t", t=WIN_TILES),
                                         dst_f[:, :].rearrange("p (w t) -> p w t", t=WIN_TILES),
                                         small[:, 0:WINS].rearrange("p (w o) -> p w o", o=1)
                                         .broadcast_to((P, WINS, WIN_TILES)), ALU.subtract))
            nc.vector.tensor_copy(row_near[:, :], small[0:1, 0:WINS])
            link(nc.vector.tensor_copy(base_f[:, :], small[:, 0:WINS]))
            nc.vector.tensor_scalar(outside[:, 0:TILES], rel_near[:, :], 0.0, None, ALU.is_lt)
            link(nc.vector.tensor_scalar(above[:, :], rel_near[:, :], float(WIN - 1), None, ALU.is_gt))
            nc.vector.tensor_tensor(outside[:, 0:TILES], outside[:, 0:TILES], above[:, :], ALU.add)
            link(nc.vector.tensor_tensor(outside[:, TILES:TILES + ORDERED], base_f[:, 2:WINS], base_f[:, 0:ORDERED],
                                         ALU.subtract))
            nc.vector.tensor_scalar(outside[:, TILES:TILES + ORDERED], outside[:, TILES:TILES + ORDERED],
                                    float(WIN), None, ALU.is_lt)
            link(nc.vector.tensor_scalar(outside[:, TILES + ORDERED:CHECKS], base_f[:, LAST_WINS:WINS],
                                         float(EARLY * P), None, ALU.is_lt))
            nc.vector.reduce_sum(outside_n[:, :], outside[:, :], AX).then_inc(s_outside, 1)
            dve.wait_ge(s_outside_sum, 1)
            nc.vector.tensor_copy(far_flag[:, :], small[0:1, 64:65]).then_inc(s_flag, 1)

            landed = {t0: (s_nodes[i], 16 if i < len(X_CUTS) - 1 else 32) for i, (t0, _) in enumerate(X_CUTS)}
            for h in range(2):
                layer_stats(nodes0, h * HALF, (h + 1) * HALF, landed)
                rstd_of(h * HALF, (h + 1) * HALF, h + 1)
                for t in range(h * HALF, (h + 1) * HALF):
                    last = nc.vector.tensor_scalar(normed0[:, t, :], nodes0[:, t, :], mv[:, t, 0:1],
                                                   rstd[:, t:t + 1], ALU.subtract, ALU.mult)
                last.then_inc(s_normed, 1)

            dve.wait_ge(s_const, 16 * 3)
            link(nc.vector.tensor_copy(rel_far[:, :], dst_f[:, :]))
            for rel in (rel_near, rel_far):
                nc.vector.memset(rel[:, FULL_TILES + 1:TILES], -1e5)
                link(nc.vector.tensor_tensor(rel[:, FULL_TILES:FULL_TILES + 1], rel[:, FULL_TILES:FULL_TILES + 1],
                                             elem[:, 1:2], ALU.add))
            dve.wait_ge(s_paths, 16 * 3)
            nc.vector.tensor_scalar(off_a[:, :], paths_sb[:, :, 0], float(EXT), None, ALU.mult)
            link(nc.vector.tensor_scalar(packed_f[:, :], paths_sb[:, :, 1], float(EXT * 65536), None, ALU.mult))
            link(nc.vector.tensor_tensor(packed_f[:, :], packed_f[:, :], off_a[:, :], ALU.add))
            link(nc.vector.tensor_copy(packed[:, :], packed_f[:, :]))
            link(nc.vector.tensor_scalar(i3_col[:, :], i3_sb[:, :], float(EIGHTH), elem[:, 0:1], ALU.mult, ALU.add))
            for c in range(CHUNKS):
                last = nc.vector.tensor_scalar(combine[:, c, :], cols[:, :], i3_col[:, c:c + 1], coef_sb[:, c:c + 1],
                                               ALU.is_equal, ALU.mult)
            last.then_inc(s_combine, 1)
            nc.vector.tensor_copy(ident_b[:, :], ident[:, :]).then_inc(s_ready, 1)

            dve.wait_ge(s_weight, 16)
            nc.vector.tensor_reduce(mx[:, 1:2], w_sb.rearrange("p a b -> p (a b)"), AX, ALU.max,
                                    apply_absolute_value=True).then_inc(s_wmax, 1)
            dve.wait_ge(s_mxT, 1)
            nc.vector.reduce_max(mx_all[:, 1:2], small[0:1, 128:256], AX).then_inc(s_mx1, 1)
            dve.wait_ge(s_mxb, 1)
            fp8_scale(1)
            weight_to_fp8()

            regs = [dve.alloc_register(f"path_{p}") for p in range(PATHS // 2)]
            ra, rb = dve.alloc_register("off_a"), dve.alloc_register("off_b")

            def windows(rel, g, b):
                nc.vector.tensor_tensor(
                    onehot[b][:, :, :],
                    rel[:, bass.ds(g * GROUP_TILES, GROUP_TILES)].rearrange("p (t o) -> p t o", o=1)
                    .broadcast_to((P, GROUP_TILES, WIN)),
                    cols[:, 0:WIN].rearrange("p (o n) -> p o n", o=1).broadcast_to((P, GROUP_TILES, WIN)),
                    ALU.is_equal).then_inc(s_onehot[b], 1)

            def load_paths(c):
                for h in range(2):
                    dve.load(regs[16 * h:16 * h + 16], packed[0:1, c * CHUNK + 16 * h:c * CHUNK + 16 * h + 16])

            def edge_pass(n, rel):
                with dve.Fori(0, PAIRS) as it:
                    k = n * PAIRS + it
                    for b in range(2):
                        load_paths(0)
                        dve.wait_ge(s_x1[b], k * (16 * GROUP_TILES) + 16 * GROUP_TILES)
                        dve.wait_ge(s_x2[b], k * 32 + 32)
                        for c in range(CHUNKS):
                            s = c % 2
                            dve.wait_ge(s_scattered[s], AHEAD + k * CHUNKS + (2 * b + c // 2))
                            if c == 0:
                                windows(rel, 2 * it + b, b)
                            for q in range(CHUNK):
                                r = regs[(c % 2) * CHUNK + q]
                                dve.reg_alu(ra, r, 0xFFFF, ALU.bitwise_and)
                                dve.reg_alu(rb, r, 16, ALU.logical_shift_right)
                                a = dve.snap(ra, min_val=0, max_val=DIM - EXT)
                                bb = dve.snap(rb, min_val=0, max_val=DIM - EXT)
                                last = nc.vector.tensor_tensor(prod[s][:, :, q, :], x1[b][:, :, bass.ds(a, EXT)],
                                                               x2[b][:, :, bass.ds(bb, EXT)], ALU.mult)
                            last.then_inc(s_prod[s], 1)
                            if c == 1:
                                load_paths(2)

            def far(p):
                dve.wait_ge(s_far, p * 3 + 2)
                dve.sem_inc(s_waited_dve, 1)
                edge_pass(p, rel_far)

            branch_on(dve, lambda: edge_pass(0, rel_near), far)

            nc.vector.memset(nodes1[96:P, NT - 1, :], 0.0).then_inc(s_zrow, 1)
            for h, (t0, t1) in enumerate(((0, EARLY), (EARLY, NT))):
                layer_stats(nodes1, t0, t1, {t0: (s_back[h], 16 * QUARTERS if h == 0 else 16)})
                rstd_of(t0, t1, 3 + h)
                nc.vector.scalar_tensor_tensor(out=shift[:, t0:t1], in0=mv[:, t0:t1, 0], scalar=-1.0,
                                               in1=rstd[:, t0:t1], op0=ALU.mult, op1=ALU.mult).then_inc(s_norm, 1)
                for t in range(t0, t1):
                    dve.wait_ge(s_y, t + 1)
                    nc.vector.tensor_reduce(mx_tile[:, t:t + 1], y[:, t, :], AX, ALU.max,
                                            apply_absolute_value=True).then_inc(s_dve, 1)
                    chain[0] += 1
            dve.wait_ge(s_dve, chain[0])
            nc.vector.reduce_max(mx[:, 0:1], mx_tile[:, :], AX).then_inc(s_wmax, 1)
            dve.wait_ge(s_mxT, 2)
            nc.vector.reduce_max(mx_all[:, 0:1], small[0:1, 128:256], AX).then_inc(s_mx1, 1)
            dve.wait_ge(s_mxb, 2)
            fp8_scale(0)
            nc.vector.scalar_tensor_tensor(out=out_scale[:, :], in0=scale_inv[:, 0:1], scalar=-1.0,
                                           in1=scale_inv[:, 1:2], op0=ALU.mult, op1=ALU.mult).then_inc(s_xscale, 1)

            def clip(i):
                ts = slice(PAIR * i, PAIR * i + PAIR)
                dve.wait_ge(s_v, i + 1)
                link(nc.vector.tensor_scalar(y[:, ts, :], y[:, ts, :], FP8_MAX, -FP8_MAX, ALU.min, ALU.max))
                nc.vector.tensor_scalar(expo[:, ts, :].bitcast(i32), y[:, ts, :].bitcast(i32), 0x7F800000, None,
                                        ALU.bitwise_and).then_inc(s_expo, 1)

            def round_pair(i):
                ts = slice(PAIR * i, PAIR * i + PAIR)
                dve.wait_ge(s_magic, i + 1)
                link(nc.vector.scalar_tensor_tensor(out=y[:, ts, :], in0=expo[:, ts, :], scalar=F32_ROUND * 2.0 ** -6,
                                                    in1=y[:, ts, :], op0=ALU.max, op1=ALU.add))
                nc.vector.scalar_tensor_tensor(out=yq[:, ts, :], in0=expo[:, ts, :], scalar=F32_ROUND * 2.0 ** -6,
                                               in1=y[:, ts, :], op0=ALU.max, op1=ALU.subtract).then_inc(s_yq, 1)

            def results(i):
                for t in range(PAIR * i, PAIR * i + PAIR):
                    dve.wait_ge(s_mm, t + 1)
                    nc.vector.scalar_tensor_tensor(out=res[:, t, :], in0=ffn_out[t % 4], scalar=out_scale[:, 0:1],
                                                   in1=nodes1[:, t, :], op0=ALU.mult, op1=ALU.add).then_inc(s_res, 1)

            clip(0)
            for i in range(NPAIRS):
                if i + 1 < NPAIRS:
                    clip(i + 1)
                round_pair(i)
                if i >= 2:
                    results(i - 2)
            for i in range(NPAIRS - 2, NPAIRS):
                results(i)

        @block.scalar
        def _(act):
            act.dma_start(src_sb[:, :], src_t).then_inc(s_src_in, 16)
            act.dma_start(ident[:, :], ident_c).then_inc(s_const, 16)
            act.dma_start(cols[:, :], cols_c).then_inc(s_const, 16)
            act.dma_start(elem[:, :], elem_c).then_inc(s_const, 16)
            act.dma_start(paths_sb[:, :, :], paths.rearrange("(o p) k -> o p k", o=1)).then_inc(s_paths, 16)
            act.dma_start(i3_sb[:, :], i3_rep).then_inc(s_paths, 16)
            act.dma_start(coef_sb[:, :], coef_rep).then_inc(s_paths, 16)

            def roots(k, t0, t1):
                act.wait_ge(s_var, k)
                cs = slice(t0, t1)
                nc.scalar.activation(std[:, cs], var_e[:, cs], ACT.Sqrt).then_inc(s_std, 1)

            roots(1, 0, HALF)
            act.wait_ge(s_normed, 1)
            act.dma_start(xn_dram[0:HALF * P, :].rearrange("(t p) c -> p t c", p=P),
                          normed0[:, 0:HALF, :]).then_inc(s_normed_out, 16)
            act.dma_start(w_sb, weight_q.rearrange("q k n -> k q n")).then_inc(s_weight, 16)
            roots(2, HALF, NT)
            act.wait_ge(s_normed, 2)
            act.dma_start(xn_dram[HALF * P:(NT - 1) * P, :].rearrange("(t p) c -> p t c", p=P),
                          normed0[:, HALF:NT - 1, :]).then_inc(s_normed_out, 16)
            act.dma_start(xn_dram[(NT - 1) * P:NODES, :], normed0[0:LAST, NT - 1, :]).then_inc(s_normed_out, 16)
            act.wait_ge(s_zero, 1)
            act.wait_ge(s_x1[0], 16 * GROUP_TILES)
            for q in range(QUARTERS):
                act.dma_start(table[q, NODES:TABLE_ROWS, :], zeros[0:WIN, :]).then_inc(s_table_init, 16)
            act.dma_start(table[:, 0:NODES, :], x_quarters).then_inc(s_table_init, 16)
            act.wait_ge(s_flag, 1)
            for ahead in (*s_sums, *s_sums_T, *s_rows):
                act.sem_inc(ahead, AHEAD)

            def edge_pass(n):
                with act.Fori(0, PAIRS) as it:
                    k = n * PAIRS + it
                    for c in range(BODY_CHUNKS + 1):
                        s = c % 2
                        if c >= 1:
                            act.wait_ge(s_turned[1 - s], k * CHUNKS + ((c - 1) // 2 + 1))
                            nc.scalar.activation(sums_T[1 - s][:, :, :], turn[1 - s][:, :, :], ACT.Copy)\
                                .then_inc(s_sums_T[1 - s], 1)
                        if c < BODY_CHUNKS:
                            act.wait_ge(s_scattered[s], AHEAD + k * CHUNKS + (c // 2 + 1))
                            nc.scalar.activation(sums[s][:, :, :], acc[s][:, :, :], ACT.Copy).then_inc(s_sums[s], 1)
                        if c in (CHUNKS, 2 * CHUNKS):
                            b = c // CHUNKS - 1
                            act.wait_ge(s_combined[b], k + 1)
                            act.wait_ge(s_rows_free[b], AHEAD + k)
                            nc.scalar.activation(rows[b][:, :, :], comb[b][:, :, :], ACT.Copy).then_inc(s_rows[b], 1)

            branch_on(act, lambda: edge_pass(0), edge_pass)

            for h, (t0, t1) in enumerate(((0, EARLY), (EARLY, NT))):
                roots(3 + h, t0, t1)
                act.wait_ge(s_norm, h + 1)
                for t in range(t0, t1):
                    nc.scalar.activation(y[:, t, :], nodes1[:, t, :], ACT.Identity, bias=shift[:, t:t + 1],
                                         scale=rstd[:, t:t + 1]).then_inc(s_y, 1)

            def scaled(i):
                ts = slice(PAIR * i, PAIR * i + PAIR)
                nc.scalar.activation(y[:, ts, :], y[:, ts, :], ACT.Copy, scale=scale[:, 0:1]).then_inc(s_v, 1)

            def magic(i):
                ts = slice(PAIR * i, PAIR * i + PAIR)
                act.wait_ge(s_expo, i + 1)
                nc.scalar.activation(expo[:, ts, :], expo[:, ts, :], ACT.Copy, scale=F32_ROUND).then_inc(s_magic, 1)

            def turned(i):
                act.wait_ge(s_yT, i + 1)
                nc.scalar.activation(yqT[:, PAIR * i:PAIR * i + PAIR, :, :], turn_b[i % 2], ACT.Copy).then_inc(s_yTc, 1)

            act.wait_ge(s_xscale, 1)
            scaled(0)
            scaled(1)
            for i in range(NPAIRS):
                magic(i)
                if i + 2 < NPAIRS:
                    scaled(i + 2)
                if i >= 1:
                    turned(i - 1)
            turned(NPAIRS - 1)

        @block.tensor
        def _(pe):
            for s in range(2):
                pe.sem_inc(s_scattered[s], AHEAD)
            pe.wait_ge(s_dstf, 1)
            nc.tensor.matmul(small[:, 0:WINS], ones[0:1, :], dst_f[0:1, 0:TILES:WIN_TILES], start=True, stop=True)\
                .then_inc(s_base, 1)
            pe.wait_ge(s_outside, 1)
            nc.tensor.matmul(small[0:1, 64:65], outside_n[:, :], ones[:, 0:1], start=True, stop=True)\
                .then_inc(s_outside_sum, 1)
            pe.wait_ge(s_const, 16 * 3)

            def spread_max(k, n):
                pe.wait_ge(s_wmax, n)
                nc.tensor.transpose(small[0:1, 128:256], mx[:, k:k + 1], ident[:, :]).then_inc(s_mxT, 1)
                pe.wait_ge(s_mx1, 2 - k)
                nc.tensor.matmul(small[:, k:k + 1], ones[0:1, :], mx_all[0:1, k:k + 1], start=True, stop=True)\
                    .then_inc(s_mxb, 1)

            pe.wait_ge(s_flag, 1)
            spread_max(1, 1)
            pe.wait_ge(s_combine, 1)
            pe.wait_ge(s_ready, 1)

            def scatter(k, b, c):
                s = c % 2
                if c == 0:
                    pe.wait_ge(s_onehot[b], k + 1)
                pe.wait_ge(s_prod[s], AHEAD + k * CHUNKS + (2 * b + c // 2 + 1))
                pe.wait_ge(s_sums[s], AHEAD + k * CHUNKS + (2 * b + c // 2))
                for t in range(GROUP_TILES):
                    for q in range(QUARTERS):
                        last = nc.tensor.matmul(acc[s][32 * q:32 * q + 32, t // WIN_TILES, :], onehot[b][:, t, :],
                                                prod[s][:, t, :, EIGHTH * q:EIGHTH * q + EIGHTH],
                                                start=(t == 0), stop=(t == GROUP_TILES - 1),
                                                skip_group_check=True)
                last.then_inc(s_scattered[s], 1)

            def turn_chunk(k, c):
                s = c % 2
                pe.wait_ge(s_sums[s], AHEAD + k * CHUNKS + (c // 2 + 1))
                pe.wait_ge(s_sums_T[s], AHEAD + k * CHUNKS + c // 2)
                for w in range(GROUP_WINS):
                    last = nc.tensor.transpose(turn[s][:, w, :], sums[s][:, w, :], ident[:, :])
                last.then_inc(s_turned[s], 1)

            def combine_chunk(k, c):
                s, b, cc = c % 2, c // CHUNKS, c % CHUNKS
                pe.wait_ge(s_sums_T[s], AHEAD + k * CHUNKS + (c // 2 + 1))
                if cc == 0:
                    pe.wait_ge(s_rows[b], AHEAD + k)
                for w in range(GROUP_WINS):
                    last = nc.tensor.matmul(comb[b][:, w, :], sums_T[s][:, w, :], combine[:, cc, :],
                                            start=(cc == 0 and w == 0), stop=(cc == CHUNKS - 1),
                                            skip_group_check=True)
                if cc == CHUNKS - 1:
                    last.then_inc(s_combined[b], 1)

            def edge_pass(n):
                with pe.Fori(0, PAIRS) as it:
                    k = n * PAIRS + it
                    for c in range(BODY_CHUNKS + 1):
                        if c >= 1:
                            turn_chunk(k, c - 1)
                        if c < BODY_CHUNKS:
                            scatter(k, c // CHUNKS, c % CHUNKS)
                        if c >= 1:
                            combine_chunk(k, c - 1)

            branch_on(pe, lambda: edge_pass(0), edge_pass)

            spread_max(0, 3)
            for i in range(NPAIRS + 1):
                if i < NPAIRS:
                    pe.wait_ge(s_yq, i + 1)
                    if i >= 2:
                        pe.wait_ge(s_yTc, i - 1)
                    for h in range(PAIR):
                        for q in range(QUARTERS):
                            last = nc.tensor.transpose(turn_b[i % 2][:, h, q, :],
                                                       yq[:, PAIR * i + h, q * P:(q + 1) * P], ident_b[:, :])
                    last.then_inc(s_yT, 1)
                if i >= 1:
                    pe.wait_ge(s_yTc, i)
                    for t in range(PAIR * (i - 1), PAIR * i):
                        if t >= 4:
                            pe.wait_ge(s_res, t - 3)
                        for q in range(QUARTERS):
                            last = nc.tensor.matmul(ffn_out[t % 4], yqT[:, t, q, :], wq[:, q, :],
                                                    start=(q == 0), stop=(q == QUARTERS - 1))
                        last.then_inc(s_mm, 1)


def kernel(x, src, dst, edge_attr_512, L0_gnn_path_coeffs, L0_gnn_path_indices, L0_ffn_weight):
    import numpy as np
    import concourse.bacc as bacc
    from concourse.bass_utils import run_bass_kernel_spmd

    x, src, dst, edges, coef, paths, weight = (np.asarray(a) for a in (
        x, src, dst, edge_attr_512, L0_gnn_path_coeffs, L0_gnn_path_indices, L0_ffn_weight))
    order = np.concatenate([np.arange(FULL_TILES * P)] + [np.arange(EDGES - P, EDGES)] * 2)
    elem = np.stack([np.arange(P) % EIGHTH, np.where(np.arange(P) < P - TAIL, -1e5, 0.0)], 1)
    arrays = {
        "x": x,
        "x_quarters": x.reshape(NODES, SEGS, QUARTERS, EIGHTH).transpose(2, 0, 1, 3).reshape(QUARTERS, NODES, QCOLS),
        "edges": edges,
        "src_t": src[order].reshape(TILES, P).T,
        "dst_t": dst[order].reshape(TILES, P).T,
        "paths": paths,
        "i3_rep": np.repeat(paths[:, 2].reshape(CHUNKS, CHUNK), EIGHTH, 1).T,
        "coef_rep": np.repeat(coef.reshape(CHUNKS, CHUNK), EIGHTH, 1).T,
        "weight_q": weight.reshape(SEGS, QUARTERS, EIGHTH, SEGS, QUARTERS, EIGHTH).transpose(1, 0, 2, 4, 3, 5)
        .reshape(QUARTERS, P, DIM),
        "ident_c": np.eye(P, dtype=np.float32),
        "cols_c": np.tile(np.arange(P, dtype=np.float32), (P, 1)),
        "elem_c": elem.astype(np.float32),
    }
    nc = bacc.Bacc("TRN2", target_bir_lowering=False, num_devices=1)
    arrays = {k: np.ascontiguousarray(a) for k, a in arrays.items()}
    aps = {k: nc.dram_tensor(k, a.shape, mybir.dt.from_np(a.dtype), kind="ExternalInput").ap()
           for k, a in arrays.items()}
    out = nc.dram_tensor("out", (NODES, DIM), mybir.dt.float32, kind="ExternalOutput").ap()
    gnn_ffn(nc, **aps, out=out)
    r = run_bass_kernel_spmd(nc, [arrays], core_ids=[0])
    return np.ascontiguousarray(r.results[0]["out"].reshape(NODES, QUARTERS, SEGS, EIGHTH).transpose(0, 2, 1, 3)
                                .reshape(NODES, DIM))
```

```python
import concourse.bass as bass
from concourse import mybir
from concourse.alu_op_type import AluOpType as ALU
from contextlib import ExitStack

NODES, EDGES, DIM, PATHS = 1250, 21250, 512, 64
SEGS, EXT = 16, 32
P = 128
QUARTERS, EIGHTH = 4, 8
QCOLS = SEGS * EIGHTH
WIN = 32
WIN_TILES, GROUP_TILES = 3, 12
GROUP_WINS = GROUP_TILES // WIN_TILES
FULL_TILES = EDGES // P
TAIL = EDGES - FULL_TILES * P
GROUPS = -(-(FULL_TILES + 1) // GROUP_TILES)
TILES = GROUPS * GROUP_TILES
WINS = TILES // WIN_TILES
PAIRS = GROUPS // 2
MAIN_TILES = 10
CHUNK = 16
CHUNKS = PATHS // CHUNK
BODY_CHUNKS = 2 * CHUNKS
AHEAD = 1
GEN_PASSES = -(-NODES // WIN)
TABLE_ROWS = NODES + WIN
NT = 10
LAST = NODES - (NT - 1) * P
HALF = NT // 2
ACT_NORMED = 7
X_CUTS = [(0, 3), (3, HALF), (HALF, 8), (8, NT)]
EARLY = NT - 1
READY = NT - 2
LAST_WINS = WINS - GROUP_WINS
STEP = 2
CHECKS = TILES + 2 * GROUP_WINS + STEP
FIRST_TILES = 6
UNITS = [(0, 1), (1, 2), (2, 4), (4, 6), (6, 8), (8, NT)]
NU = len(UNITS)
ACT_READY = READY - 2
RSQRT_GUESS = float(0x5F3759DF)
RSQRT_STEPS = 3
FP8_MAX = 448.0
F32_ROUND = 1.5 * 2.0 ** 20


def gnn_ffn(nc, x, x_quarters, edges, src_t, dst_t, paths, i3_rep, coef_rep, weight_q,
            ident_c, cols_c, elem_c, out):
    fp32, bf16, i32 = mybir.dt.float32, mybir.dt.bfloat16, mybir.dt.int32
    ACT = mybir.ActivationFunctionType
    AX = mybir.AxisListType.X

    ctx = ExitStack()
    with ctx:
        def sb(name, shape, dt=fp32):
            return ctx.enter_context(nc.sbuf_tensor(name, shape, dt))

        def pb(name, shape, dt=fp32):
            return ctx.enter_context(nc.psum_tensor(name, shape, dt))

        def sem(name):
            return ctx.enter_context(nc.semaphore(name))

        xn_dram = nc.dram_tensor("xn_dram", [NODES, DIM], fp32, kind="Internal").ap()
        table = nc.dram_tensor("sum_table", [TABLE_ROWS, DIM], fp32, kind="Internal").ap()

        x1 = [sb(f"x1_{b}", [P, GROUP_TILES, DIM]) for b in range(2)]
        x2 = [sb(f"x2_{b}", [P, GROUP_TILES, DIM]) for b in range(2)]
        prod = [sb(f"prod_{s}", [P, GROUP_TILES, CHUNK, EXT]) for s in range(2)]
        distance = sb("distance", [P, GROUP_TILES, WIN])
        rel_slot = sb("rel_slot", [P, GROUP_TILES])
        onehot = [sb(f"onehot_{b}", [P, GROUP_TILES, WIN]) for b in range(2)]
        src_slot = [sb(f"src_slot_{b}", [P, GROUP_TILES], i32) for b in range(2)]
        sums = [sb(f"sums_{s}", [P, QUARTERS, CHUNK * EIGHTH]) for s in range(2)]
        sums_T = [sb(f"sums_T_{s}", [P, QUARTERS, P]) for s in range(2)]
        rows = [sb(f"rows_{b}", [P, DIM]) for b in range(2)]
        src_sb = sb("src_sb", [P, TILES], i32)
        dst_sb = sb("dst_sb", [P, TILES], i32)
        dst_f = sb("dst_f", [P, TILES])
        rel_near = sb("rel_near", [P, TILES])
        rel_far = sb("rel_far", [P, TILES])
        base_f = sb("base_f", [P, WINS])
        outside = sb("outside", [P, CHECKS])
        above = sb("above", [P, TILES])
        outside_n = sb("outside_n", [P, 1])
        far_flag = sb("far_flag", [1, 1], i32)
        row_near = sb("row_near", [1, WINS], i32)
        row_far_f = sb("row_far_f", [1, WINS])
        row_far = sb("row_far", [1, WINS], i32)
        paths_sb = sb("paths_sb", [1, PATHS, 3], i32)
        off_a = sb("off_a", [1, PATHS])
        packed_f = sb("packed_f", [1, PATHS])
        packed = sb("packed", [1, PATHS], i32)
        i3_sb = sb("i3_sb", [P, CHUNKS], i32)
        coef_sb = sb("coef_sb", [P, CHUNKS])
        i3_col = sb("i3_col", [P, CHUNKS])
        combine = sb("combine", [P, CHUNKS, QCOLS])
        ident = sb("ident", [P, P])
        ident_b = sb("ident_b", [P, P], bf16)
        cols = sb("cols", [P, P])
        elem = sb("elem", [P, 3])
        last_at = sb("last_at", [P, GROUP_WINS])
        place = sb("place", [P, P])
        ones = sb("ones", [P, P])
        zeros = sb("zeros", [P, P])
        stats = sb("stats", [P, NT, 6])
        mv = sb("mv", [P, NT, 2])
        var_e = sb("var_e", [P, NT])
        std = sb("std", [P, NT])
        inv = sb("inv", [P, NT])
        quot = sb("quot", [P, NT])
        rstd = sb("rstd", [P, NT])
        newton = sb("newton", [P, NT])
        row_sum = sb("row_sum", [P, EARLY])
        neg_mean = sb("neg_mean", [P, EARLY])
        row_squares = sb("row_squares", [P, EARLY])
        wq = sb("wq", [P, QUARTERS, DIM], bf16)
        mx = sb("mx", [P, 2])
        mx_tile = sb("mx_tile", [P, NT])
        shift = sb("shift", [P, NT])
        mx_all = sb("mx_all", [1, 2])
        mx_bc = sb("mx_bc", [P, 2])
        mx_inv = sb("mx_inv", [P, 2])
        scale = sb("scale", [P, 2])
        scale_inv = sb("scale_inv", [P, 2])
        out_scale = sb("out_scale", [P, 1])
        nodes0 = prod[0][:, :, :, :].rearrange("p t q e -> p (t q e)")[:, 0:NT * DIM]\
            .rearrange("p (t c) -> p t c", c=DIM)
        normed0 = prod[1][:, :, :, :].rearrange("p t q e -> p (t q e)")[:, 0:NT * DIM]\
            .rearrange("p (t c) -> p t c", c=DIM)
        w_sb, w_tmp, w_exp = (sb(name, [P, QUARTERS, DIM])[:, :, :] for name in ("w_sb", "w_tmp", "w_exp"))
        nodes1 = x1[0][:, 0:NT, :]
        y = x2[0][:, 0:NT, :]
        expo = x2[1][:, 0:NT, :]
        yq = prod[0][:, :, :, :].rearrange("p t q e -> p (t q e)")[:, 0:NT * DIM // 2]\
            .bitcast(bf16).rearrange("p (t c) -> p t c", c=DIM)
        yqT = prod[0][:, :, :, :].rearrange("p t q e -> p (t q e)")[:, NT * DIM // 2:NT * DIM]\
            .bitcast(bf16).rearrange("p (t k c) -> p t k c", k=4, c=P)
        res = normed0

        acc = [pb(f"acc_{s}", [P, QUARTERS, CHUNK * EIGHTH]) for s in range(2)]
        turn = [pb(f"turn_{s}", [P, QUARTERS, P]) for s in range(2)]
        comb = [pb(f"comb_{b}", [P, QUARTERS, QCOLS]) for b in range(2)]
        small = pb("small", [P, 512])
        turn_b = [turn[s][:, :, :].rearrange("p w c -> p (w c)").bitcast(bf16)
                  .rearrange("p (t q c) -> p t q c", t=2, q=QUARTERS) for s in range(2)]
        ffn_out = [t[:, :, :].rearrange("p a b -> p (a b)") for t in (*comb, *acc)]
        last_sums = ffn_out[0]

        s_const = sem("s_const")
        s_nodes = [sem(f"s_nodes_{i}") for i in range(len(X_CUTS))]
        s_dst = sem("s_dst")
        s_src_in = sem("s_src_in")
        s_paths = sem("s_paths")
        s_weight = sem("s_weight")
        s_dve = sem("s_dve")
        s_var = sem("s_var")
        s_std = sem("s_std")
        s_row_sum = sem("s_row_sum")
        s_neg_mean = sem("s_neg_mean")
        s_row_squares = sem("s_row_squares")
        s_pool = sem("s_pool")
        s_early_norm = sem("s_early_norm")
        s_normed = sem("s_normed")
        s_normed_act = sem("s_normed_act")
        s_normed_out = sem("s_normed_out")
        s_dstf = sem("s_dstf")
        s_base = sem("s_base")
        s_outside = sem("s_outside")
        s_outside_sum = sem("s_outside_sum")
        s_flag = sem("s_flag")
        s_ready = sem("s_ready")
        s_combine = sem("s_combine")
        s_table_init = sem("s_table_init")
        s_zero = sem("s_zero")
        s_x1 = [sem(f"s_x1_{b}") for b in range(2)]
        s_x2 = [sem(f"s_x2_{b}") for b in range(2)]
        s_src = sem("s_src")
        s_rel_slot = sem("s_rel_slot")
        s_distance = sem("s_distance")
        s_onehot = [sem(f"s_onehot_{b}") for b in range(2)]
        s_prod = [sem(f"s_prod_{s}") for s in range(2)]
        s_scattered = [sem(f"s_scattered_{s}") for s in range(2)]
        s_sums = [sem(f"s_sums_{s}") for s in range(2)]
        s_turned = [sem(f"s_turned_{s}") for s in range(2)]
        s_sums_T = [sem(f"s_sums_T_{s}") for s in range(2)]
        s_combined = [sem(f"s_combined_{b}") for b in range(2)]
        s_rows = [sem(f"s_rows_{b}") for b in range(2)]
        s_added = [sem(f"s_added_{b}") for b in range(2)]
        s_rows_free = [sem(f"s_rows_free_{b}") for b in range(2)]
        s_far = sem("s_far")
        s_waited_pool = sem("s_waited_pool")
        s_waited_act = sem("s_waited_act")
        s_place = sem("s_place")
        s_placed = sem("s_placed")
        s_back = [sem(f"s_back_{h}") for h in range(2)]
        s_zrow = sem("s_zrow")
        s_wmax = sem("s_wmax")
        s_mxT = sem("s_mxT")
        s_mx1 = sem("s_mx1")
        s_mxb = sem("s_mxb")
        s_norm = sem("s_norm")
        s_y = sem("s_y")
        s_scale = sem("s_scale")
        s_out_scale = sem("s_out_scale")
        s_v = sem("s_v")
        s_expo = sem("s_expo")
        s_magic = sem("s_magic")
        s_yq = sem("s_yq")
        s_yT = sem("s_yT")
        s_yTc = sem("s_yTc")
        s_mm = sem("s_mm")
        s_res = sem("s_res")
        s_out = sem("s_out")

        block = ctx.enter_context(nc.Block())

        def branch_on(eng, near, far, far_end=None):
            flag = eng.alloc_register("flag")
            eng.load(flag, far_flag[0:1, 0:1])
            with eng.If_eq(flag, 0):
                near()
            with eng.Else():
                with eng.Fori(0, GEN_PASSES) as p:
                    far(p)
                if far_end is not None:
                    far_end()
            eng.nop()

        def rsqrt(eng, link, cs, fused):
            r, v, tmp = rstd[:, cs], var_e[:, cs], newton[:, cs]
            link(eng.tensor_scalar(r.bitcast(i32), v.bitcast(i32), -0.5, RSQRT_GUESS, ALU.mult, ALU.add))
            for _ in range(RSQRT_STEPS):
                if fused:
                    link(eng.scalar_tensor_tensor(out=tmp, in0=r, scalar=-0.5, in1=v, op0=ALU.mult, op1=ALU.mult))
                    link(eng.tensor_tensor(tmp, tmp, r, ALU.mult))
                    link(eng.scalar_tensor_tensor(out=r, in0=tmp, scalar=1.5, in1=r, op0=ALU.add, op1=ALU.mult))
                else:
                    link(eng.tensor_tensor(tmp, r, v, ALU.mult))
                    link(eng.tensor_tensor(tmp, tmp, r, ALU.mult))
                    link(eng.tensor_scalar(tmp, tmp, -0.5, 1.5, ALU.mult, ALU.add))
                    link(eng.tensor_tensor(r, tmp, r, ALU.mult))

        @block.sync
        def _(sp):
            sp.dma_start(dst_sb[:, :], dst_t).then_inc(s_dst, 16)
            for i, (t0, t1) in enumerate(X_CUTS):
                full = min(t1, NT - 1)
                sp.dma_start(nodes0[:, t0:full, :],
                             x[t0 * P:full * P, :].rearrange("(t p) c -> p t c", p=P)).then_inc(s_nodes[i], 16)
            sp.wait_ge(s_zrow, 1)
            sp.dma_start(nodes0[0:LAST, NT - 1, :], x[(NT - 1) * P:NODES, :]).then_inc(s_nodes[-1], 16)
            sp.dma_start(w_sb, weight_q.rearrange("q k n -> k q n")).then_inc(s_weight, 16)

            def load_first():
                for t0, t1 in ((0, FIRST_TILES), (FIRST_TILES, GROUP_TILES)):
                    if t0 > 0:
                        sp.wait_ge(s_normed_out, 16 * 3)
                    sp.dma_start(x2[0][:, t0:t1, :], edges[t0 * P:t1 * P, :].rearrange("(t p) c -> p t c", p=P))\
                        .then_inc(s_x2[0], 16)

            def load(g, b, tail=False):
                row = g * (GROUP_TILES * P)
                sp.dma_start(x2[b][:, 0:MAIN_TILES, :],
                             edges[bass.ds(row, MAIN_TILES * P), :].rearrange("(t p) c -> p t c", p=P))\
                    .then_inc(s_x2[b], 16)
                if not tail:
                    sp.dma_start(x2[b][:, MAIN_TILES:GROUP_TILES, :],
                                 edges[bass.ds(row + MAIN_TILES * P, 2 * P), :]
                                 .rearrange("(t p) c -> p t c", p=P)).then_inc(s_x2[b], 16)
                else:
                    sp.dma_start(x2[b][:, MAIN_TILES:GROUP_TILES, :],
                                 edges[EDGES - P:EDGES, :].rearrange("(o p) c -> p o c", o=1)
                                 .broadcast_to((P, 2, DIM))).then_inc(s_x2[b], 16)

            def edge_pass(n):
                sp.wait_ge(s_prod[1], n * (PAIRS * CHUNKS) + AHEAD)
                load_first()
                sp.wait_ge(s_x1[0], n * (16 * PAIRS * GROUP_TILES) + 16 * GROUP_TILES)
                load(1, 1)

                def step(it):
                    for b in range(2):
                        sp.wait_ge(s_prod[1], AHEAD + (n * PAIRS + it) * CHUNKS + (2 * b - 2))
                        load(2 * it + b, b)
                with sp.Fori(1, PAIRS - 1) as it:
                    step(it)
                for b in range(2):
                    sp.wait_ge(s_prod[1], AHEAD + (n * PAIRS + PAIRS - 1) * CHUNKS + (2 * b - 2))
                    load(GROUPS - 2 + b, b, tail=(b == 1))

            def table_ready():
                sp.dma_start(nodes1[:, 0:READY, :], table[0:READY * P, :].rearrange("(t p) c -> p t c", p=P))\
                    .then_inc(s_back[0], 16)

            def table_rest():
                for t in range(READY, NT):
                    n = min(P, NODES - t * P)
                    sp.dma_start(nodes1[0:n, t, :], table[t * P:t * P + n, :]).then_inc(s_back[1], 16)

            def near():
                edge_pass(0)
                sp.wait_ge(s_prod[1], AHEAD + (PAIRS - 1) * CHUNKS + CHUNKS // 2)
                sp.wait_ge(s_rows_free[1], AHEAD + PAIRS - 1)
                table_ready()
                sp.wait_ge(s_rows_free[0], AHEAD + PAIRS)
                table_rest()

            def far_end():
                sp.wait_ge(s_rows_free[1], AHEAD + GEN_PASSES * PAIRS)
                table_ready()
                table_rest()

            sp.wait_ge(s_flag, 1)
            branch_on(sp, near, edge_pass, far_end)

            for t in range(NT):
                sp.wait_ge(s_res, t + 1)
                n = P if t < NT - 1 else LAST
                sp.dma_start(out[t * P:t * P + n, :], res[0:n, t, :]).then_inc(s_out, 16)
            sp.wait_ge(s_out, 16 * NT)

        @block.gpsimd
        def _(pool):
            def take_wait():
                pool.sem_inc(s_waited_pool, 1)

            def indices(g, b):
                nc.gpsimd.tensor_copy(src_slot[b][:, :], src_sb[:, bass.ds(g * GROUP_TILES, GROUP_TILES)])\
                    .then_inc(s_src, 1)

            def gather(n, it, b):
                pool.wait_ge(s_src, (n * PAIRS + it) * 2 + (b + 1))
                take_wait()
                for t in range(GROUP_TILES):
                    nc.gpsimd.indirect_dma_start(
                        out=x1[b][:, t, :], out_offset=None, in_=xn_dram,
                        in_offset=bass.IndirectOffsetOnAxis(ap=src_slot[b][:, t:t + 1], axis=0))\
                        .then_inc(s_x1[b], 16)

            def add_rows(n, it, b, row_of, regs, steps=((0,), (1,), (2,), (3,))):
                pool.load(regs, row_of[0:1, bass.ds((2 * it + b) * GROUP_WINS, GROUP_WINS)])
                k = n * PAIRS + it
                pool.wait_ge(s_table_init, 16 * 2)
                pool.wait_ge(s_rows[b], AHEAD + k + 1)
                added = 0
                for step in steps:
                    for w in step:
                        row = pool.snap(regs[w], min_val=0, max_val=TABLE_ROWS - WIN)
                        pool.dma_start(table[bass.ds(row, WIN), :], rows[b][w * WIN:(w + 1) * WIN, :],
                                       accum_op=ALU.add).then_inc(s_added[b], 16)
                    added += len(step)
                    pool.wait_ge(s_added[b], k * (16 * GROUP_WINS) + 16 * added)
                    if added < GROUP_WINS:
                        take_wait()
                pool.sem_inc(s_rows_free[b], 1)

            chain = [0]

            def link(ins):
                chain[0] += 1
                ins.then_inc(s_pool, 1)
                pool.wait_ge(s_pool, chain[0])

            def early_norms():
                for t0, t1 in ((0, READY), (READY, EARLY)):
                    pool.wait_ge(s_row_squares, t1)
                    link(nc.gpsimd.tensor_scalar(var_e[:, t0:t1], row_squares[:, t0:t1], 1.0 / DIM, 1e-5,
                                                 ALU.mult, ALU.add))
                    rsqrt(nc.gpsimd, link, slice(t0, t1), fused=False)
                    nc.gpsimd.tensor_tensor(shift[:, t0:t1], neg_mean[:, t0:t1], rstd[:, t0:t1], ALU.mult)\
                        .then_inc(s_early_norm, 1)
                chain[0] = 0

            def edge_pass(n, row_of, regs):
                for b in range(2):
                    indices(b, b)
                    gather(n, 0, b)
                with pool.Fori(1, PAIRS) as it:
                    for b in range(2):
                        k = n * PAIRS + it
                        pool.wait_ge(s_prod[1], AHEAD + k * CHUNKS + (2 * b - 2))
                        take_wait()
                        indices(2 * it + b, b)
                        gather(n, it, b)
                        add_rows(n, it - 1, b, row_of, regs)

            for b in range(2):
                pool.sem_inc(s_rows_free[b], AHEAD)
            nc.gpsimd.memset(zeros[:, :], 0.0).then_inc(s_zero, 1)
            nc.gpsimd.memset(row_far_f[:, :], 0.0).then_inc(s_far, 1)
            pool.wait_ge(s_far, 1)
            nc.gpsimd.tensor_copy(row_far[:, :], row_far_f[:, :]).then_inc(s_far, 1)
            pool.wait_ge(s_src_in, 16)
            pool.wait_ge(s_flag, 1)
            pool.wait_ge(s_far, 2)
            pool.wait_ge(s_normed_out, 16 * 3)
            regs = [pool.alloc_register(f"row_{w}") for w in range(GROUP_WINS)]

            def near():
                edge_pass(0, row_near, regs)
                add_rows(0, PAIRS - 1, 0, row_near, regs, steps=((0, 2), (1, 3)))
                early_norms()

            def far(p):
                pool.wait_ge(s_ready, 1)
                edge_pass(p, row_far, regs)
                for b in range(2):
                    add_rows(p, PAIRS - 1, b, row_far, regs)
                nc.gpsimd.tensor_scalar(rel_far[:, :], rel_far[:, :], float(-WIN), None, ALU.add).then_inc(s_far, 1)
                nc.gpsimd.tensor_scalar(row_far_f[:, :], row_far_f[:, :], float(WIN), None, ALU.add)\
                    .then_inc(s_far, 1)
                pool.wait_ge(s_far, p * 3 + 4)
                take_wait()
                nc.gpsimd.tensor_copy(row_far[:, :], row_far_f[:, :]).then_inc(s_far, 1)
                pool.wait_ge(s_far, p * 3 + 5)

            branch_on(pool, near, far, early_norms)

        @block.vector
        def _(dve):
            chain = [0]

            def link(ins):
                chain[0] += 1
                ins.then_inc(s_dve, 1)
                dve.wait_ge(s_dve, chain[0])

            def layer_stats(nodes, t0, t1, landed=(), root=False):
                tiles = range(t0, t1)
                first = chain[0]
                for t in tiles:
                    if t in landed:
                        dve.wait_ge(*landed[t])
                    chain[0] += 1
                    nc.vector.bn_stats(stats[:, t, :], nodes[:, t, :]).then_inc(s_dve, 1)
                for i, t in enumerate(tiles):
                    dve.wait_ge(s_dve, first + i + 1)
                    chain[0] += 1
                    nc.vector.bn_aggr(mv[:, t, :], stats[:, t, :]).then_inc(s_dve, 1)
                dve.wait_ge(s_dve, chain[0])
                var = nc.vector.tensor_scalar(var_e[:, t0:t1], mv[:, t0:t1, 1], 1e-5, None, ALU.add)
                if root:
                    var.then_inc(s_var, 1)
                else:
                    link(var)

            def rstd_of(t0, t1, k):
                cs = slice(t0, t1)
                dve.wait_ge(s_std, k)
                link(nc.vector.reciprocal(inv[:, cs], std[:, cs]))
                link(nc.vector.tensor_tensor(quot[:, cs], var_e[:, cs], inv[:, cs], ALU.mult))
                link(nc.vector.tensor_tensor(quot[:, cs], quot[:, cs], std[:, cs], ALU.add))
                link(nc.vector.tensor_scalar(quot[:, cs], quot[:, cs], 0.5, None, ALU.mult))
                link(nc.vector.reciprocal(rstd[:, cs], quot[:, cs]))

            def shift_of(t0, t1):
                nc.vector.scalar_tensor_tensor(out=shift[:, t0:t1], in0=mv[:, t0:t1, 0], scalar=-1.0,
                                               in1=rstd[:, t0:t1], op0=ALU.mult, op1=ALU.mult).then_inc(s_norm, 1)

            def fp8_scale(k):
                link(nc.vector.tensor_scalar(mx_bc[:, k:k + 1], small[:, k:k + 1], 1e-12, None, ALU.max))
                link(nc.vector.reciprocal(mx_inv[:, k:k + 1], mx_bc[:, k:k + 1]))
                nc.vector.tensor_scalar(scale[:, k:k + 1], mx_inv[:, k:k + 1], FP8_MAX, None, ALU.mult)\
                    .then_inc(s_scale, 1)
                dve.wait_ge(s_scale, 2 - k)
                link(nc.vector.reciprocal(scale_inv[:, k:k + 1], scale[:, k:k + 1]))

            def weight_to_fp8():
                link(nc.vector.tensor_scalar(w_tmp, w_sb, scale[:, 1:2], FP8_MAX, ALU.mult, ALU.min))
                link(nc.vector.tensor_scalar(w_tmp, w_tmp, -FP8_MAX, None, ALU.max))
                link(nc.vector.tensor_scalar(w_exp.bitcast(i32), w_tmp.bitcast(i32), 0x7F800000, None,
                                             ALU.bitwise_and))
                link(nc.vector.tensor_scalar(w_exp, w_exp, 2.0 ** -6, F32_ROUND, ALU.max, ALU.mult))
                link(nc.vector.tensor_tensor(w_tmp, w_tmp, w_exp, ALU.add))
                nc.vector.tensor_tensor(wq[:, :, :], w_tmp, w_exp, ALU.subtract).then_inc(s_wmax, 1)

            for s in range(2):
                dve.sem_inc(s_prod[s], AHEAD)
            nc.vector.memset(nodes0[96:P, NT - 1, :], 0.0).then_inc(s_zrow, 1)
            link(nc.vector.memset(ones[:, :], 1.0))
            dve.wait_ge(s_dst, 16)
            nc.vector.tensor_copy(dst_f[:, :], dst_sb[:, :]).then_inc(s_dstf, 1)
            dve.wait_ge(s_base, 1)
            link(nc.vector.tensor_tensor(rel_near[:, :].rearrange("p (w t) -> p w t", t=WIN_TILES),
                                         dst_f[:, :].rearrange("p (w t) -> p w t", t=WIN_TILES),
                                         small[:, 0:WINS].rearrange("p (w o) -> p w o", o=1)
                                         .broadcast_to((P, WINS, WIN_TILES)), ALU.subtract))
            nc.vector.tensor_copy(row_near[:, :], small[0:1, 0:WINS])
            link(nc.vector.tensor_copy(base_f[:, :], small[:, 0:WINS]))
            nc.vector.tensor_scalar(outside[:, 0:TILES], rel_near[:, :], 0.0, None, ALU.is_lt)
            link(nc.vector.tensor_scalar(above[:, :], rel_near[:, :], float(WIN - 1), None, ALU.is_gt))
            nc.vector.tensor_tensor(outside[:, 0:TILES], outside[:, 0:TILES], above[:, :], ALU.add)
            behind = outside[:, TILES + 2 * GROUP_WINS:CHECKS]
            link(nc.vector.tensor_tensor(behind, base_f[:, LAST_WINS - STEP:LAST_WINS],
                                         base_f[:, LAST_WINS - 2 * STEP:LAST_WINS - STEP], ALU.subtract))
            nc.vector.tensor_scalar(behind, behind, float(WIN), None, ALU.is_lt)
            last_but_one = outside[:, TILES:TILES + GROUP_WINS]
            last_group = outside[:, TILES + GROUP_WINS:TILES + 2 * GROUP_WINS]
            nc.vector.tensor_scalar(last_but_one, base_f[:, LAST_WINS - GROUP_WINS:LAST_WINS], float(READY * P), None,
                                    ALU.is_lt)
            link(nc.vector.tensor_scalar(last_group, base_f[:, LAST_WINS:WINS], float(EARLY * P), None, ALU.is_lt))
            nc.vector.reduce_sum(outside_n[:, :], outside[:, :], AX).then_inc(s_outside, 1)
            dve.wait_ge(s_outside_sum, 1)
            nc.vector.tensor_copy(far_flag[:, :], small[0:1, 64:65]).then_inc(s_flag, 1)

            landed = {t0: (s_nodes[i], 16 if i < len(X_CUTS) - 1 else 32) for i, (t0, _) in enumerate(X_CUTS)}
            for h in range(2):
                layer_stats(nodes0, h * HALF, (h + 1) * HALF, landed, root=True)
                rstd_of(h * HALF, (h + 1) * HALF, h + 1)
                shift_of(h * HALF, (h + 1) * HALF)
            for t in range(ACT_NORMED, NT):
                last = nc.vector.tensor_scalar(normed0[:, t, :], nodes0[:, t, :], mv[:, t, 0:1],
                                               rstd[:, t:t + 1], ALU.subtract, ALU.mult)
            last.then_inc(s_normed, 1)

            dve.wait_ge(s_const, 16 * 3)
            link(nc.vector.tensor_copy(rel_far[:, :], dst_f[:, :]))
            for rel in (rel_near, rel_far):
                nc.vector.memset(rel[:, FULL_TILES + 1:TILES], -1e5)
                link(nc.vector.tensor_tensor(rel[:, FULL_TILES:FULL_TILES + 1], rel[:, FULL_TILES:FULL_TILES + 1],
                                             elem[:, 1:2], ALU.add))
            dve.wait_ge(s_paths, 16 * 3)
            nc.vector.tensor_scalar(off_a[:, :], paths_sb[:, :, 0], float(EXT), None, ALU.mult)
            link(nc.vector.tensor_scalar(packed_f[:, :], paths_sb[:, :, 1], float(EXT * 65536), None, ALU.mult))
            link(nc.vector.tensor_tensor(packed_f[:, :], packed_f[:, :], off_a[:, :], ALU.add))
            link(nc.vector.tensor_copy(packed[:, :], packed_f[:, :]))
            link(nc.vector.tensor_scalar(i3_col[:, :], i3_sb[:, :], float(EIGHTH), elem[:, 0:1], ALU.mult, ALU.add))
            for c in range(CHUNKS):
                last = nc.vector.tensor_scalar(combine[:, c, :], cols[:, :], i3_col[:, c:c + 1], coef_sb[:, c:c + 1],
                                               ALU.is_equal, ALU.mult)
            last.then_inc(s_combine, 1)
            link(nc.vector.tensor_scalar(last_at[:, :], base_f[:, LAST_WINS:WINS], elem[:, 2:3], None, ALU.add))
            for w in range(GROUP_WINS):
                ps = slice(w * WIN, (w + 1) * WIN)
                last = nc.vector.tensor_scalar(place[ps, :], cols[ps, :], last_at[ps, w:w + 1], None, ALU.is_equal)
            last.then_inc(s_place, 1)
            nc.vector.memset(mx_tile[:, :], 0.0)
            nc.vector.tensor_copy(ident_b[:, :], ident[:, :]).then_inc(s_ready, 1)

            dve.wait_ge(s_weight, 16)
            nc.vector.tensor_reduce(mx[:, 1:2], w_sb.rearrange("p a b -> p (a b)"), AX, ALU.max,
                                    apply_absolute_value=True).then_inc(s_wmax, 1)
            dve.wait_ge(s_mxT, 1)
            nc.vector.reduce_max(mx_all[:, 1:2], small[0:1, 128:256], AX).then_inc(s_mx1, 1)
            dve.wait_ge(s_mxb, 1)
            fp8_scale(1)
            weight_to_fp8()

            regs = [dve.alloc_register(f"path_{p}") for p in range(PATHS // 2)]
            ra, rb = dve.alloc_register("off_a"), dve.alloc_register("off_b")

            def load_paths(c):
                for h in range(2):
                    dve.load(regs[16 * h:16 * h + 16], packed[0:1, c * CHUNK + 16 * h:c * CHUNK + 16 * h + 16])

            def group(k, b, tiles=GROUP_TILES):
                load_paths(0)
                dve.wait_ge(s_x1[b], k * (16 * GROUP_TILES) + 16 * GROUP_TILES)
                dve.wait_ge(s_x2[b], k * 32 + 32)
                for c in range(CHUNKS):
                    s = c % 2
                    dve.wait_ge(s_scattered[s], AHEAD + k * CHUNKS + (2 * b + c // 2))
                    for q in range(CHUNK):
                        r = regs[(c % 2) * CHUNK + q]
                        dve.reg_alu(ra, r, 0xFFFF, ALU.bitwise_and)
                        dve.reg_alu(rb, r, 16, ALU.logical_shift_right)
                        a = dve.snap(ra, min_val=0, max_val=DIM - EXT)
                        bb = dve.snap(rb, min_val=0, max_val=DIM - EXT)
                        last = nc.vector.tensor_tensor(prod[s][:, 0:tiles, q, :], x1[b][:, 0:tiles, bass.ds(a, EXT)],
                                                       x2[b][:, 0:tiles, bass.ds(bb, EXT)], ALU.mult)
                    last.then_inc(s_prod[s], 1)
                    if c == 1:
                        load_paths(2)

            def edge_pass(n):
                with dve.Fori(0, PAIRS - 1) as it:
                    for b in range(2):
                        group(n * PAIRS + it, b)
                group(n * PAIRS + (PAIRS - 1), 0)
                group(n * PAIRS + (PAIRS - 1), 1, GROUP_TILES - 1)

            branch_on(dve, lambda: edge_pass(0), edge_pass)

            def row_max(t, n):
                chain[0] += 1
                nc.vector.tensor_reduce(mx_tile[0:n, t:t + 1], y[0:n, t, :], AX, ALU.max,
                                        apply_absolute_value=True).then_inc(s_dve, 1)

            dve.wait_ge(s_early_norm, 1)
            for t in range(ACT_READY, READY):
                chain[0] += 1
                nc.vector.tensor_scalar(y[:, t, :], nodes1[:, t, :], rstd[:, t:t + 1], shift[:, t:t + 1],
                                        ALU.mult, ALU.add).then_inc(s_dve, 1)
            own = chain[0]
            for t in range(ACT_READY):
                if t == ACT_READY // 2:
                    dve.wait_ge(s_dve, own)
                    for t1 in range(ACT_READY, READY):
                        row_max(t1, P)
                dve.wait_ge(s_y, t + 1)
                row_max(t, P)
            dve.wait_ge(s_y, ACT_READY + 1)
            row_max(READY, P)
            dve.wait_ge(s_placed, 1)
            link(nc.vector.tensor_tensor(nodes1[0:LAST, NT - 1, :], nodes1[0:LAST, NT - 1, :], last_sums[0:LAST, :],
                                         ALU.add))
            layer_stats(nodes1, EARLY, NT)
            rsqrt(nc.vector, link, slice(EARLY, NT), fused=True)
            link(nc.vector.tensor_scalar(y[:, EARLY, :], nodes1[:, EARLY, :], mv[:, EARLY, 0:1],
                                         rstd[:, EARLY:NT], ALU.subtract, ALU.mult))
            row_max(EARLY, LAST)
            dve.wait_ge(s_dve, chain[0])
            nc.vector.reduce_max(mx[:, 0:1], mx_tile[:, :], AX).then_inc(s_wmax, 1)
            dve.wait_ge(s_mxT, 2)
            nc.vector.reduce_max(mx_all[:, 0:1], small[0:1, 128:256], AX).then_inc(s_mx1, 1)
            dve.wait_ge(s_mxb, 2)
            fp8_scale(0)
            nc.vector.scalar_tensor_tensor(out=out_scale[:, :], in0=scale_inv[:, 0:1], scalar=-1.0,
                                           in1=scale_inv[:, 1:2], op0=ALU.mult, op1=ALU.mult).then_inc(s_out_scale, 1)
            dve.wait_ge(s_out_scale, 1)

            def exponents(i):
                ts = slice(*UNITS[i])
                dve.wait_ge(s_v, i + 1)
                nc.vector.tensor_scalar(expo[:, ts, :].bitcast(i32), y[:, ts, :].bitcast(i32), 0x7F800000, None,
                                        ALU.bitwise_and).then_inc(s_expo, 1)

            def round_unit(i):
                ts = slice(*UNITS[i])
                dve.wait_ge(s_magic, i + 1)
                link(nc.vector.scalar_tensor_tensor(out=y[:, ts, :], in0=expo[:, ts, :], scalar=F32_ROUND * 2.0 ** -6,
                                                    in1=y[:, ts, :], op0=ALU.max, op1=ALU.add))
                link(nc.vector.scalar_tensor_tensor(out=yq[:, ts, :], in0=expo[:, ts, :], scalar=F32_ROUND * 2.0 ** -6,
                                                    in1=y[:, ts, :], op0=ALU.max, op1=ALU.subtract))
                nc.vector.tensor_scalar(yq[:, ts, :], yq[:, ts, :], FP8_MAX, -FP8_MAX, ALU.min, ALU.max)\
                    .then_inc(s_yq, 1)

            def results(i):
                for t in range(*UNITS[i]):
                    dve.wait_ge(s_mm, t + 1)
                    nc.vector.scalar_tensor_tensor(out=res[:, t, :], in0=ffn_out[t % 4], scalar=out_scale[:, 0:1],
                                                   in1=nodes1[:, t, :], op0=ALU.mult, op1=ALU.add).then_inc(s_res, 1)

            exponents(0)
            for i in range(NU):
                if i + 1 < NU:
                    exponents(i + 1)
                round_unit(i)
                if i >= 2:
                    results(i - 2)
            for i in range(NU - 2, NU):
                results(i)

        @block.scalar
        def _(act):
            act.dma_start(src_sb[:, :], src_t).then_inc(s_src_in, 16)
            act.dma_start(ident[:, :], ident_c).then_inc(s_const, 16)
            act.dma_start(cols[:, :], cols_c).then_inc(s_const, 16)
            act.dma_start(elem[:, :], elem_c).then_inc(s_const, 16)
            act.dma_start(paths_sb[:, :, :], paths.rearrange("(o p) k -> o p k", o=1)).then_inc(s_paths, 16)
            act.dma_start(i3_sb[:, :], i3_rep).then_inc(s_paths, 16)
            act.dma_start(coef_sb[:, :], coef_rep).then_inc(s_paths, 16)

            def roots(k, t0, t1):
                act.wait_ge(s_var, k)
                cs = slice(t0, t1)
                nc.scalar.activation(std[:, cs], var_e[:, cs], ACT.Sqrt).then_inc(s_std, 1)

            def scaled_and_shifted(out, nodes, t):
                return nc.scalar.activation(out[:, t, :], nodes[:, t, :], ACT.Identity, bias=shift[:, t:t + 1],
                                            scale=rstd[:, t:t + 1])

            for h, t1 in enumerate((HALF, ACT_NORMED)):
                roots(h + 1, h * HALF, (h + 1) * HALF)
                act.wait_ge(s_norm, h + 1)
                for t in range(h * HALF, t1):
                    scaled_and_shifted(normed0, nodes0, t).then_inc(s_normed_act, 1)
                act.wait_ge(s_normed_act, t1)
                if h == 0:
                    act.dma_start(xn_dram[0:HALF * P, :].rearrange("(t p) c -> p t c", p=P),
                                  normed0[:, 0:HALF, :]).then_inc(s_normed_out, 16)
            act.wait_ge(s_normed, 1)
            act.dma_start(xn_dram[HALF * P:(NT - 1) * P, :].rearrange("(t p) c -> p t c", p=P),
                          normed0[:, HALF:NT - 1, :]).then_inc(s_normed_out, 16)
            act.dma_start(xn_dram[(NT - 1) * P:NODES, :], normed0[0:LAST, NT - 1, :]).then_inc(s_normed_out, 16)
            act.wait_ge(s_zero, 1)
            act.wait_ge(s_x1[0], 16 * GROUP_TILES)
            act.dma_start(table[NODES:TABLE_ROWS, :].rearrange("n (q c) -> (n q) c", c=P), zeros[:, :])\
                .then_inc(s_table_init, 16)
            act.dma_start(table[0:NODES, :], x_quarters).then_inc(s_table_init, 16)
            act.wait_ge(s_flag, 1)
            for ahead in (*s_sums, *s_sums_T, *s_rows):
                act.sem_inc(ahead, AHEAD)

            def take_wait():
                act.sem_inc(s_waited_act, 1)

            def windows(rel, k, it, b):
                g = 2 * it + b
                nc.scalar.activation(rel_slot[:, :], rel[:, bass.ds(g * GROUP_TILES, GROUP_TILES)], ACT.Copy)\
                    .then_inc(s_rel_slot, 1)
                act.wait_ge(s_rel_slot, 2 * k + b + 1)
                take_wait()
                for t in range(GROUP_TILES):
                    nc.scalar.activation(distance[:, t, :], cols[:, 0:WIN], ACT.Abs, bias=rel_slot[:, t:t + 1],
                                         scale=-1.0).then_inc(s_distance, 1)
                act.wait_ge(s_distance, (2 * k + b + 1) * GROUP_TILES)
                take_wait()
                nc.scalar.activation(onehot[b][:, :, :], distance[:, :, :], ACT.Relu, bias=1.0, scale=-1.0)\
                    .then_inc(s_onehot[b], 1)

            def body(rel, k, it, last=False, between=()):
                for c in range(BODY_CHUNKS + 1):
                    s = c % 2
                    if c >= 1:
                        act.wait_ge(s_turned[1 - s], k * CHUNKS + ((c - 1) // 2 + 1))
                        nc.scalar.activation(sums_T[1 - s][:, :, :], turn[1 - s][:, :, :], ACT.Copy)\
                            .then_inc(s_sums_T[1 - s], 1)
                    if c < BODY_CHUNKS:
                        act.wait_ge(s_scattered[s], AHEAD + k * CHUNKS + (c // 2 + 1))
                        nc.scalar.activation(sums[s][:, :, :], acc[s][:, :, :], ACT.Copy).then_inc(s_sums[s], 1)
                    if c == BODY_CHUNKS and c in between:
                        between[c]()
                    if c in (CHUNKS, 2 * CHUNKS):
                        b = c // CHUNKS - 1
                        act.wait_ge(s_combined[b], k + 1)
                        act.wait_ge(s_rows_free[b], AHEAD + k)
                        nc.scalar.activation(rows[b][:, :], comb[b][:, :, :].rearrange("p q c -> p (q c)"),
                                             ACT.Copy).then_inc(s_rows[b], 1)
                    if c == 1:
                        windows(rel, k, it, 1)
                    if c == CHUNKS + 1 and not last:
                        windows(rel, k + 1, it + 1, 0)
                    if c < BODY_CHUNKS and c in between:
                        between[c]()

            def means(t0, t1):
                for t in range(t0, t1):
                    nc.scalar.activation(y[:, t, :], nodes1[:, t, :], ACT.Copy, accum_out=row_sum[:, t:t + 1])\
                        .then_inc(s_row_sum, 1)
                act.wait_ge(s_row_sum, t1)
                nc.scalar.activation(neg_mean[:, t0:t1], row_sum[:, t0:t1], ACT.Copy, scale=-1.0 / DIM)\
                    .then_inc(s_neg_mean, 1)

            def squares(t0, t1):
                act.wait_ge(s_neg_mean, 1 if t1 <= READY else 2)
                for t in range(t0, t1):
                    nc.scalar.activation(y[:, t, :], nodes1[:, t, :], ACT.Square, bias=neg_mean[:, t:t + 1],
                                         accum_out=row_squares[:, t:t + 1]).then_inc(s_row_squares, 1)

            def early_tiles(t0, t1):
                act.wait_ge(s_early_norm, 1 if t1 <= READY else 2)
                for t in range(t0, t1):
                    scaled_and_shifted(y, nodes1, t).then_inc(s_y, 1)

            def stats_ready():
                act.wait_ge(s_back[0], 16)
                means(0, READY)

            def stats_rest():
                act.wait_ge(s_back[1], 16 * (NT - READY))
                means(READY, EARLY)
                squares(READY, EARLY)

            def edge_pass(rel, n, between=()):
                windows(rel, n * PAIRS, 0, 0)
                with act.Fori(0, PAIRS - 1) as it:
                    body(rel, n * PAIRS + it, it)
                body(rel, n * PAIRS + (PAIRS - 1), PAIRS - 1, last=True, between=between)

            def near():
                def behind_sixth():
                    stats_rest()
                    early_tiles(0, ACT_READY - 1)

                edge_pass(rel_near, 0, {CHUNKS - 1: stats_ready,
                                        CHUNKS: lambda: squares(0, READY // 2),
                                        CHUNKS + 1: lambda: squares(READY // 2, READY),
                                        CHUNKS + 2: behind_sixth,
                                        CHUNKS + 3: lambda: early_tiles(ACT_READY - 1, ACT_READY),
                                        BODY_CHUNKS: lambda: early_tiles(READY, EARLY)})

            def far(p):
                act.wait_ge(s_far, p * 3 + 2)
                take_wait()
                edge_pass(rel_far, p)

            def far_end():
                stats_ready()
                squares(0, READY)
                stats_rest()
                early_tiles(0, ACT_READY)
                early_tiles(READY, EARLY)

            act.wait_ge(s_ready, 1)
            branch_on(act, near, far, far_end)

            def scaled(i):
                ts = slice(*UNITS[i])
                nc.scalar.activation(y[:, ts, :], y[:, ts, :], ACT.Copy, scale=scale[:, 0:1]).then_inc(s_v, 1)

            def magic(i):
                ts = slice(*UNITS[i])
                act.wait_ge(s_expo, i + 1)
                nc.scalar.activation(expo[:, ts, :], expo[:, ts, :], ACT.Copy, scale=F32_ROUND).then_inc(s_magic, 1)

            def turned(i):
                act.wait_ge(s_yT, i + 1)
                t0, t1 = UNITS[i]
                nc.scalar.activation(yqT[:, t0:t1, :, :], turn_b[i % 2][:, 0:t1 - t0, :, :], ACT.Copy)\
                    .then_inc(s_yTc, 1)

            act.wait_ge(s_scale, 2)
            scaled(0)
            scaled(1)
            for i in range(NU):
                magic(i)
                if i + 2 < NU:
                    scaled(i + 2)
                if i >= 1:
                    turned(i - 1)
            turned(NU - 1)

        @block.tensor
        def _(pe):
            for s in range(2):
                pe.sem_inc(s_scattered[s], AHEAD)
            pe.wait_ge(s_dstf, 1)
            nc.tensor.matmul(small[:, 0:WINS], ones[0:1, :], dst_f[0:1, 0:TILES:WIN_TILES], start=True, stop=True)\
                .then_inc(s_base, 1)
            pe.wait_ge(s_outside, 1)
            nc.tensor.matmul(small[0:1, 64:65], outside_n[:, :], ones[:, 0:1], start=True, stop=True)\
                .then_inc(s_outside_sum, 1)
            pe.wait_ge(s_const, 16 * 3)

            def spread_max(k, n):
                pe.wait_ge(s_wmax, n)
                nc.tensor.transpose(small[0:1, 128:256], mx[:, k:k + 1], ident[:, :]).then_inc(s_mxT, 1)
                pe.wait_ge(s_mx1, 2 - k)
                nc.tensor.matmul(small[:, k:k + 1], ones[0:1, :], mx_all[0:1, k:k + 1], start=True, stop=True)\
                    .then_inc(s_mxb, 1)

            pe.wait_ge(s_flag, 1)
            spread_max(1, 1)
            pe.wait_ge(s_combine, 1)
            pe.wait_ge(s_ready, 1)

            def scatter(k, b, c):
                s = c % 2
                if c == 0:
                    pe.wait_ge(s_onehot[b], k + 1)
                pe.wait_ge(s_prod[s], AHEAD + k * CHUNKS + (2 * b + c // 2 + 1))
                pe.wait_ge(s_sums[s], AHEAD + k * CHUNKS + (2 * b + c // 2))
                for i in range(WIN_TILES):
                    for w in range(GROUP_WINS):
                        t = w * WIN_TILES + i
                        last = nc.tensor.matmul(acc[s][w * WIN:(w + 1) * WIN, :, :], onehot[b][:, t, :],
                                                prod[s][:, t, :, :].rearrange("p k (q u) -> p q k u", q=QUARTERS),
                                                start=(i == 0), stop=(i == WIN_TILES - 1),
                                                skip_group_check=True)
                last.then_inc(s_scattered[s], 1)

            def turn_chunk(k, c):
                s = c % 2
                pe.wait_ge(s_sums[s], AHEAD + k * CHUNKS + (c // 2 + 1))
                pe.wait_ge(s_sums_T[s], AHEAD + k * CHUNKS + c // 2)
                for q in range(QUARTERS):
                    last = nc.tensor.transpose(turn[s][:, q, :], sums[s][:, q, :], ident[:, :])
                last.then_inc(s_turned[s], 1)

            def combine_chunk(k, c):
                s, b, cc = c % 2, c // CHUNKS, c % CHUNKS
                pe.wait_ge(s_sums_T[s], AHEAD + k * CHUNKS + (c // 2 + 1))
                if cc == 0:
                    pe.wait_ge(s_rows[b], AHEAD + k)
                for q in range(QUARTERS):
                    last = nc.tensor.matmul(comb[b][:, q, :], sums_T[s][:, q, :], combine[:, cc, :],
                                            start=(cc == 0 and q == 0), stop=(cc == CHUNKS - 1),
                                            skip_group_check=True)
                if cc == CHUNKS - 1:
                    last.then_inc(s_combined[b], 1)

            def edge_pass(n):
                with pe.Fori(0, PAIRS) as it:
                    k = n * PAIRS + it
                    for c in range(BODY_CHUNKS + 1):
                        if c >= 1:
                            turn_chunk(k, c - 1)
                        if c < BODY_CHUNKS:
                            scatter(k, c // CHUNKS, c % CHUNKS)
                        if c >= 1:
                            combine_chunk(k, c - 1)

            def near():
                edge_pass(0)
                pe.wait_ge(s_rows[1], AHEAD + PAIRS)
                pe.wait_ge(s_place, 1)
                nc.tensor.matmul(last_sums, place[:, :], rows[1][:, :], start=True, stop=True).then_inc(s_placed, 1)

            def far_end():
                pe.wait_ge(s_zero, 1)
                pe.wait_ge(s_rows[1], AHEAD + GEN_PASSES * PAIRS)
                nc.tensor.matmul(last_sums, zeros[:, :], zeros[:, 0:1].broadcast_to((P, DIM)), start=True, stop=True)\
                    .then_inc(s_placed, 1)

            branch_on(pe, near, edge_pass, far_end)

            spread_max(0, 3)
            for i in range(NU + 1):
                if i >= 1:
                    pe.wait_ge(s_yTc, i)
                    for t in range(*UNITS[i - 1]):
                        if t >= len(ffn_out):
                            pe.wait_ge(s_res, t - len(ffn_out) + 1)
                        for q in range(QUARTERS):
                            last = nc.tensor.matmul(ffn_out[t % len(ffn_out)], yqT[:, t, q, :], wq[:, q, :],
                                                    start=(q == 0), stop=(q == QUARTERS - 1))
                        last.then_inc(s_mm, 1)
                if i < NU:
                    pe.wait_ge(s_yq, i + 1)
                    t0, t1 = UNITS[i]
                    for t in range(t0, t1):
                        for q in range(QUARTERS):
                            last = nc.tensor.transpose(turn_b[i % 2][:, t - t0, q, :], yq[:, t, q * P:(q + 1) * P],
                                                       ident_b[:, :])
                    last.then_inc(s_yT, 1)


def kernel(x, src, dst, edge_attr_512, L0_gnn_path_coeffs, L0_gnn_path_indices, L0_ffn_weight):
    import numpy as np
    import concourse.bacc as bacc
    from concourse.bass_utils import run_bass_kernel_spmd

    x, src, dst, edges, coef, paths, weight = (np.asarray(a) for a in (
        x, src, dst, edge_attr_512, L0_gnn_path_coeffs, L0_gnn_path_indices, L0_ffn_weight))
    order = np.concatenate([np.arange(FULL_TILES * P)] + [np.arange(EDGES - P, EDGES)] * 2)
    elem = np.stack([np.arange(P) % EIGHTH, np.where(np.arange(P) < P - TAIL, -1e5, 0.0),
                     np.arange(P) % WIN - EARLY * P], 1)
    arrays = {
        "x": x,
        "x_quarters": x.reshape(NODES, SEGS, QUARTERS, EIGHTH).transpose(0, 2, 1, 3).reshape(NODES, DIM),
        "edges": edges,
        "src_t": src[order].reshape(TILES, P).T,
        "dst_t": dst[order].reshape(TILES, P).T,
        "paths": paths,
        "i3_rep": np.repeat(paths[:, 2].reshape(CHUNKS, CHUNK), EIGHTH, 1).T,
        "coef_rep": np.repeat(coef.reshape(CHUNKS, CHUNK), EIGHTH, 1).T,
        "weight_q": weight.reshape(SEGS, QUARTERS, EIGHTH, SEGS, QUARTERS, EIGHTH).transpose(1, 0, 2, 4, 3, 5)
        .reshape(QUARTERS, P, DIM),
        "ident_c": np.eye(P, dtype=np.float32),
        "cols_c": np.tile(np.arange(P, dtype=np.float32), (P, 1)),
        "elem_c": elem.astype(np.float32),
    }
    nc = bacc.Bacc("TRN2", target_bir_lowering=False, num_devices=1)
    arrays = {k: np.ascontiguousarray(a) for k, a in arrays.items()}
    aps = {k: nc.dram_tensor(k, a.shape, mybir.dt.from_np(a.dtype), kind="ExternalInput").ap()
           for k, a in arrays.items()}
    out = nc.dram_tensor("out", (NODES, DIM), mybir.dt.float32, kind="ExternalOutput").ap()
    gnn_ffn(nc, **aps, out=out)
    r = run_bass_kernel_spmd(nc, [arrays], core_ids=[0])
    return np.ascontiguousarray(r.results[0]["out"].reshape(NODES, QUARTERS, SEGS, EIGHTH).transpose(0, 2, 1, 3)
                                .reshape(NODES, DIM))
```
